# Optimizing a Trainium2 kernel written in Bass

```python
import numpy as np
import jax
import jax.numpy as jnp

def _softmax(x, axis=-1):
    return jax.nn.softmax(x, axis=axis)

def _gelu(x):
    return jax.nn.gelu(x, approximate=True)

def _silu(x):
    return jax.nn.silu(x)

def _sigmoid(x):
    return jax.nn.sigmoid(x)

def _layernorm(x, axis=-1, eps=1e-05):
    m = jnp.mean(x, axis=axis, keepdims=True)
    v = jnp.var(x, axis=axis, keepdims=True)
    return (x - m) / jnp.sqrt(v + eps)

def _scatter_add(tgt, idx, src, axis=0):
    return tgt.at[idx].add(src)

def _segment_sum(src, seg, n):
    return jax.ops.segment_sum(src, seg, n)
kernel_name = 'mk_cond_resid_d2_seqx_r2_18782c'

def setup_inputs(seed: int=0):
    np.random.seed(seed)
    _w = jnp.asarray

    def _rec_inputs():
        import jax
        import jax.numpy as jnp
        _rk = jax.random.key(seed)
        x = 7.22e-05 + 1 * jax.random.normal(jax.random.fold_in(_rk, 1), (64, 128, 512), jnp.float32)
        _lenS = 128 - jax.random.randint(jax.random.fold_in(_rk, 7), (64,), 0, max(1, 128 // 4) + 1, jnp.int32)
        _lenS2 = 128 - jax.random.randint(jax.random.fold_in(_rk, 8), (64,), 0, max(1, 128 // 4) + 1, jnp.int32)
        cond_512 = 0.0061147 + 1.02565 * jax.random.normal(jax.random.fold_in(_rk, 11), (64, 256), jnp.float32)
        return (x, cond_512)
    x, cond_512 = _rec_inputs()

    def _L0_cond_setup():
        import jax, jax.numpy as jnp
        import numpy as np
        import math
        HEAD_NUM = 16
        EPS = 1e-08

        def modulated_linear(x, s, aff_w, aff_b, w, b):
            style = s @ aff_w.T + aff_b
            w_mod = w[None, :, :] * style[:, None, :]
            demod = jax.lax.rsqrt(jnp.sum(w_mod * w_mod, axis=2) + EPS)
            w_mod = w_mod * demod[:, :, None]
            return jnp.einsum('bni,boi->bno', x, w_mod) + b
        key = jax.random.key(seed)
        ks = jax.random.split(key, 6)
        B, N, F, S = (8, 512, 512, 256)
        return {'x': jax.random.normal(ks[0], (B, N, F), dtype=jnp.float32), 's': jax.random.normal(ks[1], (B, S), dtype=jnp.float32), 'k_aff_w': jax.random.normal(ks[2], (F, S), dtype=jnp.float32) * 0.02, 'k_aff_b': jnp.ones((F,), dtype=jnp.float32), 'k_w': jax.random.normal(ks[3], (F, F), dtype=jnp.float32) * 0.02, 'k_b': jnp.zeros((F,), dtype=jnp.float32), 'o_aff_w': jax.random.normal(ks[4], (F, S), dtype=jnp.float32) * 0.02, 'o_aff_b': jnp.ones((F,), dtype=jnp.float32), 'o_w': jax.random.normal(ks[5], (F, F), dtype=jnp.float32) * 0.02, 'o_b': jnp.zeros((F,), dtype=jnp.float32)}
    _L0_cond_all = _L0_cond_setup()
    _L0_cond_in = {k: v for k, v in _L0_cond_all.items() if k in ('k_aff_w', 'k_aff_b', 'k_w', 'k_b', 'o_aff_w', 'o_aff_b', 'o_w', 'o_b')}
    del _L0_cond_all

    def _L1_cond_setup():
        import jax, jax.numpy as jnp
        import numpy as np
        IN_DIM = 512
        OUT_DIM = 512
        MU_DIM = 256
        K = 30
        key = jax.random.key(seed)
        k1, k2, k3, k4, k5 = jax.random.split(key, 5)
        B, S = (16, 1024)
        x = jax.random.normal(k1, (B, S, IN_DIM), dtype=jnp.float32)
        mu = jax.random.normal(k2, (B, MU_DIM), dtype=jnp.float32)
        W_dec = jax.random.normal(k3, (MU_DIM, (IN_DIM + 1) * K), dtype=jnp.float32) / np.sqrt(MU_DIM)
        b_dec = jax.random.normal(k4, ((IN_DIM + 1) * K,), dtype=jnp.float32) * 0.01
        V = jax.random.normal(k5, (K, OUT_DIM), dtype=jnp.float32) / np.sqrt(K)
        return {'x': x, 'mu': mu, 'W_dec': W_dec, 'b_dec': b_dec, 'V': V}
    _L1_cond_all = _L1_cond_setup()
    _L1_cond_in = {k: v for k, v in _L1_cond_all.items() if k in ('W_dec', 'b_dec', 'V')}
    del _L1_cond_all
    return {'x': x, 'cond_512': cond_512, 'L0_cond_k_aff_w': _L0_cond_in['k_aff_w'], 'L0_cond_k_aff_b': _L0_cond_in['k_aff_b'], 'L0_cond_k_w': _L0_cond_in['k_w'], 'L0_cond_k_b': _L0_cond_in['k_b'], 'L0_cond_o_aff_w': _L0_cond_in['o_aff_w'], 'L0_cond_o_aff_b': _L0_cond_in['o_aff_b'], 'L0_cond_o_w': _L0_cond_in['o_w'], 'L0_cond_o_b': _L0_cond_in['o_b'], 'L1_cond_W_dec': _L1_cond_in['W_dec'], 'L1_cond_b_dec': _L1_cond_in['b_dec'], 'L1_cond_V': _L1_cond_in['V']}

def reference(x, cond_512, L0_cond_k_aff_w, L0_cond_k_aff_b, L0_cond_k_w, L0_cond_k_b, L0_cond_o_aff_w, L0_cond_o_aff_b, L0_cond_o_w, L0_cond_o_b, L1_cond_W_dec, L1_cond_b_dec, L1_cond_V):
    import jax
    import jax.numpy as jnp

    def _L0_cond_ref(x, s, k_aff_w, k_aff_b, k_w, k_b, o_aff_w, o_aff_b, o_w, o_b):
        import jax, jax.numpy as jnp
        import numpy as np
        import math
        HEAD_NUM = 16
        EPS = 1e-08

        def modulated_linear(x, s, aff_w, aff_b, w, b):
            style = s @ aff_w.T + aff_b
            w_mod = w[None, :, :] * style[:, None, :]
            demod = jax.lax.rsqrt(jnp.sum(w_mod * w_mod, axis=2) + EPS)
            w_mod = w_mod * demod[:, :, None]
            return jnp.einsum('bni,boi->bno', x, w_mod) + b
        B, N, F = x.shape
        H = HEAD_NUM
        D = F // H
        kx = modulated_linear(x, s, k_aff_w, k_aff_b, k_w, k_b)
        kx = kx.reshape(B, N, H, D)
        q = k = v = kx
        scores = jnp.einsum('bnhd,bnjd->bnhj', q, k) / math.sqrt(D)
        A = jax.nn.softmax(scores, axis=-1)
        out = jnp.einsum('bnhj,bnjd->bnhd', A, v).reshape(B, N, F)
        out = modulated_linear(out, s, o_aff_w, o_aff_b, o_w, o_b)
        return out

    def _L1_cond_ref(x, mu, W_dec, b_dec, V):
        import jax, jax.numpy as jnp
        import numpy as np
        IN_DIM = 512
        OUT_DIM = 512
        MU_DIM = 256
        K = 30
        B = mu.shape[0]
        U = (mu @ W_dec + b_dec).reshape(B, IN_DIM + 1, K)
        param = jnp.einsum('bik,kj->bij', U, V)
        weight = param[:, :-1, :]
        bias = param[:, -1, :]
        out = jnp.einsum('bsd,bde->bse', x, weight)
        out = out + bias[:, None, :]
        return out
    x = x + _L0_cond_ref(x, cond_512, L0_cond_k_aff_w, L0_cond_k_aff_b, L0_cond_k_w, L0_cond_k_b, L0_cond_o_aff_w, L0_cond_o_aff_b, L0_cond_o_w, L0_cond_o_b)
    x = x + _L1_cond_ref(x, cond_512, L1_cond_W_dec, L1_cond_b_dec, L1_cond_V)
    return x

_drawn_inputs = setup_inputs


def setup_inputs(seed=0):
    import zlib

    import numpy as np

    out = dict(_drawn_inputs(seed))
    spreads = {'L0_cond_k_aff_b': (1.0, 0.2),
     'L0_cond_k_b': (0.0, 0.1),
     'L0_cond_o_aff_b': (1.0, 0.2),
     'L0_cond_o_b': (0.0, 0.1)}
    factors = {'L1_cond_b_dec': 5.886}
    for name, (base, spread) in spreads.items():
        noise = np.random.default_rng([zlib.crc32(name.encode()), seed]).standard_normal(out[name].shape)
        drawn = base * np.exp(spread * noise) if base else spread * noise
        out[name] = jnp.asarray(drawn.astype(out[name].dtype))
    for name, factor in factors.items():
        out[name] = (out[name] * factor).astype(out[name].dtype)
    return out
```

```python
import concourse.bass as bass
from concourse import mybir
from contextlib import ExitStack


def cond_resid_kernel(
    nc: bass.Bass,
    x: bass.AP,
    cond: bass.AP,
    k_aff_w: bass.AP,
    k_aff_b: bass.AP,
    k_w: bass.AP,
    k_b: bass.AP,
    o_aff_w: bass.AP,
    o_aff_b: bass.AP,
    o_w: bass.AP,
    o_b: bass.AP,
    W_dec: bass.AP,
    b_dec: bass.AP,
    V: bass.AP,
    out: bass.AP,
):
    f32 = mybir.dt.float32
    f32r = mybir.dt.float32r
    bf16 = mybir.dt.bfloat16
    ALU = mybir.AluOpType
    ACT = mybir.ActivationFunctionType
    AX = mybir.AxisListType

    B, N, F = x.shape
    S = cond.shape[1]
    K = V.shape[0]
    H = 16
    D = F // H
    P = 128
    Q = 4
    T = B // Q
    KT = F // P
    ST = S // P
    TOK = Q * N
    GG = N // 8
    E = 2 * H
    KP = 32
    SCALE = float(D) ** -0.5
    EPS = 1e-8
    BIG = 1e30
    COLS = H * N
    SK, DK, SO, DO = range(4)
    NPAR = 4 * KT * Q

    ctx = ExitStack()
    with ctx:
        def sb(name, shape, dt=f32):
            return ctx.enter_context(nc.sbuf_tensor(name, shape, dt))

        def sem(name):
            return ctx.enter_context(nc.semaphore(name))

        arena = sb("arena", [P, 8192 + 8 * 2048 + 2048 + 4096])
        at = [0]

        def cut(n):
            at[0] += n
            return arena[:, at[0] - n:at[0]]

        blockdiag = cut(8192)
        kn = cut(2048)
        kq = cut(2048)
        vt = cut(2048)
        pr = cut(2048)
        aq = cut(2048)
        an = cut(2048)
        x1t = cut(2048)
        y2 = cut(1024)
        ob = cut(1024)
        xtok = cut(2048)
        xtb = cut(4096)

        bd = blockdiag.rearrange("p (c m) -> p c m", c=Q)
        bd_scores = blockdiag.rearrange("p (q e c g) -> p q e c g", q=Q, e=E, c=4)
        bd_probs = blockdiag.rearrange("p (c g q e) -> p c g q e", c=Q, g=GG, q=Q)
        kn_v = kn.rearrange("p (m q n) -> p m q n", m=KT, q=Q)
        kq_v = kq.rearrange("p (e c g) -> p e c g", e=E, c=4)
        kq_s = kq.rearrange("p (m k n) -> p m k n", m=KT, k=4)
        v_v = vt.rearrange("p (g q d) -> p g q d", g=GG, q=Q)
        aq_v = aq.rearrange("p (e c g) -> p e c g", e=E, c=4)
        aq_s = aq.rearrange("p (m k n) -> p m k n", m=KT, k=4)
        an_v = an.rearrange("p (m q n) -> p m q n", m=KT, q=Q)
        x1_v = x1t.rearrange("p (m q n) -> p m q n", m=KT, q=Q)
        y2_v = y2.rearrange("p (s f) -> p s f", s=2)
        ob_v = ob.rearrange("p (s f) -> p s f", s=2)
        xtok_v = xtok.rearrange("p (q f) -> p q f", q=Q)
        xtb_v = xtb.rearrange("p (s m q n) -> p s m q n", s=2, m=KT, q=Q)

        hi = sb("hi", [P, KT, TOK], f32r)
        lo = sb("lo", [P, KT, TOK], f32r)
        w_hi = [sb(f"w_hi{n}", [P, KT, F], f32r) for n in range(2)]
        w_lo = [sb(f"w_lo{n}", [P, KT, F], f32r) for n in range(2)]
        md = sb("md", [P, GG * Q, 32], f32r)
        rmax = sb("rmax", [P, GG * Q])
        par = sb("par", [P, T, NPAR])
        pst = sb("pst", [P, 2, NPAR])
        ubias = sb("ubias", [P, T])
        ub_st = sb("ub_st", [P, 2])
        ust = sb("ust", [P, 2, KT, Q, KP])
        zt = sb("zt", [P, N])
        kp = sb("kp", [P, 4, E, GG])
        v_rep = sb("v_rep", [P, F])
        ident = sb("ident", [P, P])
        eye32 = sb("eye32", [P, 32])
        ones_bd = sb("ones_bd", [P, P])
        neg_bd = sb("neg_bd", [P, P], f32r)
        mask_l = sb("mask_l", [2, P], bf16)
        mask_r = sb("mask_r", [2, TOK], bf16)
        aff_b = sb("aff_b", [P, 2, KT])
        bias = sb("bias", [P, 2, KT])
        bdec = sb("bdec", [P, KT, K])
        wlast = sb("wlast", [P, ST, KP])
        blast = sb("blast", [P, 1])
        ct = sb("ct", [P, ST, B])
        sty2 = sb("sty2", [P, 2, KT, B])
        cond_sb = sb("cond_sb", [B, S])

        spare = kp[:, :, :, :].rearrange("p c e g -> p (c e g)")
        dem, root, inv = (spare[:, n * 2 * KT * B:(n + 1) * 2 * KT * B].rearrange("p (w n) -> p w n", w=2)
                          for n in range(3))
        wc = [arena[:, s:s + ST * P * K].rearrange("p (m i k) -> p m i k", m=ST, k=K) for s in (0, 8192)]
        aff_in = xtb[:, 0:2048].rearrange("p (w t s) -> p w t s", w=2, t=KT)
        aff_t = xtb[:, 2048:4096].rearrange("p (w s f) -> p w s f", w=2, s=ST)
        w_in = [aq.rearrange("p (t i) -> p t i", t=KT), an.rearrange("p (t i) -> p t i", t=KT)]
        w_sq = [x1t.rearrange("p (t o) -> p t o", t=KT),
                arena[:, 8192 + 7 * 2048:8192 + 8 * 2048].rearrange("p (t o) -> p t o", t=KT)]
        us = [a.rearrange("p (t q k) -> p t q k", t=T, q=Q) for a in (aq, an)]

        u_dram = nc.dram_tensor("u_scratch", [T, P, KT, Q, KP], f32)

        Gp = ctx.enter_context(nc.psum_tensor("Gp", [P, 4, TOK], f32))
        Wp = ctx.enter_context(nc.psum_tensor("Wp", [P, 4, TOK], f32))

        def g_bank(j):
            return Gp[:, j, :]

        def w_bank(j):
            return Wp[:, j, :]

        ld_cond, ld_aff, ld_w, ld_small, ld_v = (sem(n) for n in ("ld_cond", "ld_aff", "ld_w", "ld_small", "ld_v"))
        ld_wc = [sem("ld_wc0"), sem("ld_wc1")]
        st_u = [sem("st_u0"), sem("st_u1")]
        cst = sem("cst")
        cst_part = sem("cst_part")
        zeroed = sem("zeroed")
        pe_ct, act_ct = sem("pe_ct"), sem("act_ct")
        pe_aff, act_aff = sem("pe_aff"), sem("act_aff")
        pe_sty, dve_sty, act_sty = sem("pe_sty"), sem("dve_sty"), sem("act_sty")
        pe_w, act_whi, act_wsq, dve_wlo = sem("pe_w"), sem("act_whi"), sem("act_wsq"), sem("dve_wlo")
        pe_dem, dve_dem = sem("pe_dem"), sem("dve_dem")
        dve_sum, act_root, dve_newton = sem("dve_sum"), sem("act_root"), sem("dve_newton")
        dve_rec = sem("dve_rec")
        pe_ul, act_ul = sem("pe_ul"), sem("act_ul")
        pe_u, dve_u, dve_pad = sem("pe_u"), sem("dve_u"), sem("dve_pad")
        x_in = sem("x_in")
        u_in = [sem("u_in0"), sem("u_in1")]
        k_moved, a_moved = sem("k_moved"), sem("a_moved")
        stored = [sem("stored0"), sem("stored1")]
        pe_t, pe_q, pe_s, pe_m, pe_d, pe_v, pe_pv, pe_o, pe_z, pe_y, pe_x = (
            sem(n) for n in ("pe_t", "pe_q", "pe_s", "pe_m", "pe_d", "pe_v", "pe_pv", "pe_o", "pe_z", "pe_y", "pe_x"))
        act_hi, act_xtb, act_k, act_v, act_exp, act_aq, act_ahi, act_z, act_y = (
            sem(n) for n in ("act_hi", "act_xtb", "act_k", "act_v", "act_exp", "act_aq", "act_ahi", "act_z", "act_y"))
        dve_lo, dve_max, dve_div, dve_bp, dve_bs, dve_alo, dve_x1, dve_out, dve_kp = (
            sem(n) for n in ("dve_lo", "dve_max", "dve_div", "dve_bp", "dve_bs", "dve_alo", "dve_x1", "dve_out", "dve_kp"))
        pool_md, pool_par, pool_ub = sem("pool_md"), sem("pool_par"), sem("pool_ub")

        def steps(eng, body):
            for t in (-1, 0, 1):
                body(t, t % 2, True, t >= 0, t >= 1)
            with eng.Fori(1, T // 2 - 1) as pair:
                body(2 * pair, 0, True, True, True)
                body(2 * pair + 1, 1, True, True, True)
            for t in (T - 2, T - 1, T):
                body(t, t % 2, t < T - 1, t < T, True)

        block = ctx.enter_context(nc.Block())

        @block.sync
        def _(sp):
            sp.dma_start(cond_sb[:, :], cond[:, :]).then_inc(ld_cond, 16)
            for w, a in enumerate((k_aff_w, o_aff_w)):
                sp.dma_start(aff_in[:, w], a.rearrange("(t p) s -> p t s", p=P)).then_inc(ld_aff, 16)
            for w, a in enumerate((k_aff_b, o_aff_b)):
                sp.dma_start(aff_b[:, w, :], a.rearrange("(t p) -> p t", p=P),
                             allow_slow_non_contiguous=True).then_inc(ld_small, 16)
            for w, a in enumerate((k_w, o_w)):
                sp.dma_start(w_in[w], a.rearrange("(t p) i -> p t i", p=P)).then_inc(ld_w, 16)
            sp.dma_start(xtok_v, x[0:Q].rearrange("q n f -> n q f")).then_inc(x_in, 16)
            for it in range(KT):
                if it >= 2:
                    sp.wait_ge(pe_u, 4 * (it - 1))
                sp.dma_start(wc[it % 2], W_dec[:, it * P * K:(it + 1) * P * K]
                             .rearrange("(m p) (i k) -> p m i k", p=P, k=K)).then_inc(ld_wc[it % 2], 16)
            for it in range(KT):
                sp.wait_ge(dve_u, 4 * (it + 1))
                sp.dma_start(u_dram[:, :, it, :, :].rearrange("t p q k -> p t q k"), us[it % 2])\
                  .then_inc(st_u[it % 2], 16)
            for n in range(2):
                sp.wait_ge(st_u[n], 32)

            def body(t, par, nxt, cur, prev):
                static = type(t) is int
                at_once = (lambda v: v) if static else sp.to_reg
                z_of_2nd_last = at_once(t - 1)
                t_of_next, k_of_next = at_once(4 * (t + 2)), at_once(4 * (t + 2))
                steps_made, tiles_made = at_once(t + 1), at_once(4 * (t + 1))
                tiles_before = at_once(4 * t)
                outs = [at_once(4 * (t - 1) + b + 1) for b in range(Q)]
                if cur:
                    if not static or t >= 2:
                        sp.wait_ge(pe_z, z_of_2nd_last)
                    sp.dma_start(ust[:, par], u_dram[t]).then_inc(u_in[par], 16)
                if nxt:
                    if not static or t < T - 2:
                        sp.wait_ge(pe_t, t_of_next)
                        sp.dma_start(xtok_v, x[bass.ds(Q * (t + 2), Q)].rearrange("q n f -> n q f")).then_inc(x_in, 16)
                    sp.wait_ge(act_k, k_of_next)
                    if cur:
                        sp.wait_ge(dve_bs, steps_made)
                        sp.wait_ge(dve_kp, steps_made)
                    for k in range(4):
                        for q in range(Q):
                            sp.dma_start(kq_s[D * q:D * (q + 1), :, k, :], kn_v[D * k:D * (k + 1), :, q, :])\
                              .then_inc(k_moved, 16)
                if cur:
                    sp.wait_ge(act_aq, tiles_made)
                    if prev:
                        sp.wait_ge(act_ahi, tiles_before)
                        sp.wait_ge(dve_alo, tiles_before)
                    for k in range(4):
                        for q in range(Q):
                            sp.dma_start(an_v[D * k:D * (k + 1), :, q, :], aq_s[D * q:D * (q + 1), :, k, :])\
                              .then_inc(a_moved, 16)
                if prev:
                    for b in range(Q):
                        sp.wait_ge(dve_out, outs[b])
                        sp.dma_start(out[Q * (t - 1) + b], ob_v[:, b % 2, :]).then_inc(stored[b % 2], 16)

            steps(sp, body)
            for n in range(2):
                sp.wait_ge(stored[n], 16 * 2 * T)

        @block.gpsimd
        def _(pool):
            pool.memset(ident[:, :], 0.0).then_inc(cst_part, 1)
            pool.memset(ones_bd[:, :], 0.0).then_inc(cst_part, 1)
            pool.memset(neg_bd[:, :].bitcast(f32), 0.0).then_inc(cst_part, 1)
            pool.memset(mask_l[:, :], 0.0).then_inc(cst_part, 1)
            pool.memset(mask_r[:, :], -BIG).then_inc(cst_part, 1)
            pool.memset(wlast[:, :, :], 0.0).then_inc(cst_part, 1)
            pool.memset(blast[:, :], 0.0).then_inc(cst_part, 1)
            pool.wait_ge(cst_part, 7)
            pool.affine_select(out=ident[:, :], in_=ident[:, :], compare_op=ALU.not_equal, fill=1.0, base=0,
                               pattern=[[-1, P]], channel_multiplier=1).then_inc(cst_part, 1)
            for m, fill in ((mask_l, 1.0), (mask_r, 0.0)):
                v = m[:, :].rearrange("k (a e) -> k a e", e=2)
                pool.affine_select(out=v, in_=v, compare_op=ALU.not_equal, fill=fill, base=0,
                                   pattern=[[0, v.shape[1]], [-1, 2]], channel_multiplier=1).then_inc(cst_part, 1)
            pool.wait_ge(cst_part, 10)
            for q in range(Q):
                r = slice(32 * q, 32 * (q + 1))
                pool.memset(ones_bd[r, r], 1.0).then_inc(cst, 1)
                pool.memset(neg_bd[r, r].bitcast(f32), -1.0).then_inc(cst, 1)
                pool.tensor_copy(eye32[r, :], ident[r, r]).then_inc(cst, 1)
            for w, a in enumerate((k_b, o_b)):
                pool.dma_start(bias[:, w, :], a.rearrange("(t p) -> p t", p=P),
                             allow_slow_non_contiguous=True).then_inc(ld_v, 16)
            pool.dma_start(wlast[:, :, 0:K], W_dec[:, F * K:(F + 1) * K].rearrange("(m p) k -> p m k", p=P))\
                .then_inc(ld_v, 16)
            pool.dma_start(bdec[:, :, :], b_dec[0:F * K].rearrange("(t p k) -> p t k", p=P, k=K)).then_inc(ld_v, 16)
            for q in range(Q):
                pool.dma_start(blast[KP * q:KP * q + K, :], b_dec[F * K:(F + 1) * K].rearrange("(k a) -> k a", a=1))\
                    .then_inc(ld_v, 16)
                pool.dma_start(v_rep[KP * q:KP * q + K, :], V[:, :]).then_inc(ld_v, 16)
            pool.wait_ge(pe_u, 12)
            pool.memset(blockdiag, 0.0).then_inc(zeroed, 1)

            pool.wait_ge(dve_sty, 2)
            pool.wait_ge(dve_dem, 2)
            pool.wait_ge(act_ul, 1)

            def body(t, par, nxt, cur, prev):
                if nxt:
                    if prev:
                        pool.wait_ge(dve_x1, 4 * t)
                    pool.tensor_copy(pst[:, 1 - par, :], par_all[:, bass.ds(t + 1, 1), :].rearrange("p a n -> p (a n)"))\
                        .then_inc(pool_par, 1)

            par_all = par

            def maxima(t, par, nxt, cur, prev):
                if cur:
                    if type(t) is not int or t >= 2:
                        pool.wait_ge(act_z, t - 1)
                    pool.tensor_copy(ub_st[:, par:par + 1], ubias[:, bass.ds(t, 1)]).then_inc(pool_ub, 1)
                    for j in range(4):
                        pool.wait_ge(dve_max, 4 * t + j + 1)
                        if prev:
                            pool.wait_ge(pe_m, 4 * (t - 1) + j + 1)
                        r = slice(16 * j, 16 * (j + 1))
                        pool.tensor_tensor(md[:, r, :], rmax[:, r].unsqueeze(2).to_broadcast([P, 16, 32]),
                                           eye32[:, :].unsqueeze(1).to_broadcast([P, 16, 32]), ALU.mult)\
                            .then_inc(pool_md, 1)

            def both(*a):
                maxima(*a)
                body(*a)

            steps(pool, both)

        @block.tensor
        def _(pe):
            pe.wait_ge(cst_part, 10)
            pe.wait_ge(cst, 12)
            pe.wait_ge(ld_cond, 16)
            for s in range(ST):
                last = pe.transpose(w_bank(0)[:, s * B:(s + 1) * B], cond_sb[:, s * P:(s + 1) * P], ident[0:B, 0:B])
            last.then_inc(pe_ct, 1)
            pe.wait_ge(ld_aff, 32)
            for w in range(2):
                for s in range(ST):
                    for f in range(KT):
                        last = pe.transpose(g_bank(2 * w + s)[:, f * P:(f + 1) * P],
                                            aff_in[:, w, f, s * P:(s + 1) * P], ident[:, :])
                    last.then_inc(pe_aff, 1)
            pe.wait_ge(act_ct, 1)
            pe.wait_ge(act_aff, 4)
            for w in range(2):
                for f in range(KT):
                    for s in range(ST):
                        last = pe.matmul(w_bank(1 + w)[:, f * B:(f + 1) * B], aff_t[:, w, s, f * P:(f + 1) * P],
                                         ct[:, s, :], start=(s == 0), stop=(s == ST - 1))
                last.then_inc(pe_sty, 1)
            pe.wait_ge(ld_w, 32)
            for w in range(2):
                for i in range(KT):
                    if w == 1 and i in (1, 2):
                        pe.wait_ge(dve_sty, 2)
                        pe.wait_ge(act_sty, 2)
                    for o in range(KT):
                        last = pe.transpose((w_bank if w else g_bank)(i)[:, o * P:(o + 1) * P],
                                            w_in[w][:, o, i * P:(i + 1) * P], ident[:, :])
                    last.then_inc(pe_w, 1)
            pe.wait_ge(act_sty, 2)
            for w in range(2):
                pe.wait_ge(act_wsq, 4 * (w + 1))
                pe.wait_ge(dve_wlo, 4)
                pe.wait_ge(act_whi, 4)
                for o in range(KT):
                    for i in range(KT):
                        last = pe.matmul(g_bank(w)[:, o * B:(o + 1) * B], w_sq[w][:, i, o * P:(o + 1) * P],
                                         sty2[:, w, i, :], start=(i == 0), stop=(i == KT - 1))
                last.then_inc(pe_dem, 1)
            pe.wait_ge(ld_v, 16 * (4 + 2 * Q))
            for q in range(Q):
                for s in range(ST):
                    last = pe.matmul(g_bank(2)[KP * q:KP * (q + 1), 0:T], wlast[:, s, :],
                                     ct[:, s, :].rearrange("p (t q) -> p t q", q=Q)[:, :, q],
                                     start=(s == 0), stop=(s == ST - 1))
            last.then_inc(pe_ul, 1)
            pe.wait_ge(dve_wlo, 8)
            pe.wait_ge(act_whi, 8)
            pe.wait_ge(act_wsq, 8)
            for it in range(KT):
                pe.wait_ge(ld_wc[it % 2], 16 * (it // 2 + 1))
                for n in range(4):
                    if it:
                        pe.wait_ge(dve_u, 4 * (it - 1) + n + 1)
                    for k in range(8 * n, min(8 * n + 8, K)):
                        for s in range(ST):
                            last = pe.matmul(w_bank(n)[:, (k % 8) * B:(k % 8 + 1) * B], wc[it % 2][:, s, :, k],
                                             ct[:, s, :], start=(s == 0), stop=(s == ST - 1))
                    last.then_inc(pe_u, 1)

            def project(w, m, done):
                for i in range(KT):
                    for n, (a, b) in enumerate(((w_hi, hi), (w_hi, lo), (w_lo, hi))):
                        last = pe.matmul(w_bank(m), a[w][:, i, m * P:(m + 1) * P], b[:, i, :],
                                         start=(i == 0 and n == 0), stop=(i == KT - 1 and n == 2))
                last.then_inc(done, 1)

            def body(t, par, nxt, cur, prev):
                static = type(t) is int
                if cur:
                    pe.wait_ge(dve_kp, t + 1)
                    pe.wait_ge(dve_bs, t + 1)
                    for j in range(4):
                        if prev:
                            pe.wait_ge(act_aq, 4 * (t - 1) + j + 1)
                        pe.matmul(g_bank(j), mask_l[:, :], mask_r[:, :], start=True, stop=False,
                                  skip_group_check=True)
                        for g in range(4 * j, 4 * j + 4):
                            for c in range(4):
                                last = pe.matmul(g_bank(j)[32 * c:32 * (c + 1), (g % 4) * P:(g % 4 + 1) * P],
                                                 kp[:, c, :, g], bd_scores[:, :, :, c, g],
                                                 start=False, stop=False, skip_group_check=True)
                        last.then_inc(pe_s, 1)

                def out_projection(m):
                    if not static or t >= 2:
                        if m % 2:
                            pe.wait_ge(act_y, 4 * (t - 1))
                        else:
                            pe.wait_ge(dve_out, 4 * (t - 1))
                    elif not m:
                        pe.wait_ge(act_k, 4 * (t + 1))
                    if static and t == 1 and m:
                        pe.wait_ge(act_k, 4 * (t + 1))
                    pe.wait_ge(act_ahi, 4 * t)
                    pe.wait_ge(dve_alo, 4 * t)
                    project(1, m, pe_o)

                if prev:
                    out_projection(0)
                    out_projection(1)
                if cur:
                    for j in range(4):
                        pe.wait_ge(pool_md, 4 * t + j + 1)
                        pe.matmul(g_bank(j), neg_bd[:, :], md[:, 16 * j:16 * (j + 1), :].rearrange("p a e -> p (a e)"),
                                  start=False, stop=True, skip_group_check=True).then_inc(pe_m, 1)
                if prev:
                    out_projection(2)
                    out_projection(3)
                if nxt:
                    pe.wait_ge(x_in, 16 * (t + 2))
                    for i in range(KT):
                        if prev:
                            pe.wait_ge(dve_x1, 4 * (t - 1) + i + 1)
                        elif cur:
                            pe.wait_ge(act_k, 4 * (t + 1))
                        else:
                            pe.wait_ge(dve_u, 16)
                        for q in range(Q):
                            last = pe.transpose(w_bank(i)[:, q * N:(q + 1) * N], xtok_v[:, q, i * P:(i + 1) * P],
                                                ident[:, :])
                        last.then_inc(pe_t, 1)
                if cur:
                    for j in range(4):
                        pe.wait_ge(act_exp, 4 * t + j + 1)
                        pe.matmul(g_bank(j), ones_bd[:, :], pr[:, 512 * j:512 * (j + 1)], start=True, stop=True)\
                            .then_inc(pe_d, 1)
                    for j in range(4):
                        if nxt:
                            pe.wait_ge(act_xtb, 4 * (t + 1) + j + 1)
                            pe.wait_ge(dve_lo, 4 * (t + 1) + j + 1)
                        elif prev:
                            pe.wait_ge(dve_x1, 4 * (t - 1) + j + 1)
                        for g in range(4 * j, 4 * j + 4):
                            last = pe.transpose(w_bank(j)[:, (g % 4) * P:(g % 4 + 1) * P],
                                                kp[:, :, :, g].rearrange("p c e -> p (c e)"),
                                                ident[:, :])
                        last.then_inc(pe_v, 1)
                if nxt:
                    pe.wait_ge(act_hi, 4 * (t + 2))
                    pe.wait_ge(dve_lo, 4 * (t + 2))
                    for m in range(4):
                        if cur:
                            pe.wait_ge(act_v, 4 * t + m + 1)
                        else:
                            pe.wait_ge(act_xtb, 4 * (t + 1) + m + 1)
                        project(0, m, pe_q)
                if cur:
                    pe.wait_ge(act_v, 4 * (t + 1))
                    pe.wait_ge(dve_bp, t + 1)
                    for j in range(4):
                        for g in range(4 * j, 4 * j + 4):
                            for q in range(Q):
                                last = pe.matmul(g_bank(j)[32 * q:32 * (q + 1), (g % 4) * P:(g % 4 + 1) * P],
                                                 v_v[:, g, q, :], bd_probs[:, :, g, q, :], start=True, stop=True)
                        last.then_inc(pe_pv, 1)
                if prev:
                    pe.wait_ge(dve_x1, 4 * t)
                    if static:
                        pe.wait_ge(u_in[1 - par], 16 * ((t - 1) // 2 + 1))
                    else:
                        pe.wait_ge(u_in[1 - par], 8 * (t + (1 if par else 0)))
                    if nxt:
                        pe.wait_ge(act_k, 4 * (t + 2))
                    elif cur:
                        pe.wait_ge(act_v, 4 * (t + 1))
                    for i in range(KT):
                        for q in range(Q):
                            last = pe.matmul(w_bank(0)[KP * q:KP * (q + 1), 0:N], ust[:, 1 - par, i, q, :],
                                             x1_v[:, i, q, :], start=(i == 0), stop=(i == KT - 1))
                    last.then_inc(pe_z, 1)
                    pe.wait_ge(act_z, t)
                    for b in range(Q):
                        if b >= 2:
                            pe.wait_ge(act_y, 4 * (t - 1) + b - 1)
                        pe.matmul(w_bank(1 + 2 * (b % 2)), zt[KP * b:KP * b + K, :], v_rep[KP * b:KP * b + K, :],
                                  start=True, stop=True).then_inc(pe_y, 1)
                        if b >= 2:
                            pe.wait_ge(dve_out, 4 * (t - 1) + b - 1)
                        for i in range(KT):
                            last = pe.transpose(w_bank((2, 0)[b % 2])[:, i * P:(i + 1) * P], x1_v[:, i, b, :],
                                                ident[:, :])
                        last.then_inc(pe_x, 1)

            steps(pe, body)

        @block.scalar
        def _(act):
            act.wait_ge(pe_ct, 1)
            act.activation(ct[:, :, :].rearrange("p s b -> p (s b)"), w_bank(0)[:, 0:ST * B], ACT.Copy)\
                .then_inc(act_ct, 1)
            for n in range(4):
                act.wait_ge(pe_aff, n + 1)
                act.activation(aff_t[:, n // 2, n % 2, :], g_bank(n), ACT.Copy).then_inc(act_aff, 1)
            act.wait_ge(ld_small, 32)
            for w in range(2):
                act.wait_ge(pe_sty, w + 1)
                for f in range(KT):
                    last = act.activation(sty2[:, w, f, :], w_bank(1 + w)[:, f * B:(f + 1) * B], ACT.Square,
                                          bias=aff_b[:, w, f:f + 1])
                last.then_inc(act_sty, 1)
            for w in range(2):
                for i in range(KT):
                    act.wait_ge(pe_w, 4 * w + i + 1)
                    bank = (w_bank if w else g_bank)(i)
                    act.activation(w_hi[w][:, i, :], bank, ACT.Copy).then_inc(act_whi, 1)
                    act.activation(w_sq[w][:, i, :], bank, ACT.Square).then_inc(act_wsq, 1)
            for w in range(2):
                act.wait_ge(dve_sum, w + 1)
                act.activation(root[:, w, :], dem[:, w, :], ACT.Sqrt).then_inc(act_root, 1)
            act.wait_ge(pe_ul, 1)
            act.wait_ge(ld_v, 16 * (4 + 2 * Q))
            act.activation(ubias[:, :], g_bank(2)[:, 0:T], ACT.Identity, bias=blast[:, :]).then_inc(act_ul, 1)

            def factor(par_, kind, i, q):
                n = (kind * KT + i) * Q + q
                return pst[:, par_, n:n + 1]

            def body(t, par, nxt, cur, prev):
                if prev:
                    act.wait_ge(a_moved, 256 * t)
                    act.wait_ge(pe_q, 4 * (t + 1) if cur else 4 * t)
                    for i in range(KT):
                        for q in range(Q):
                            last = act.activation(hi[:, i, q * N:(q + 1) * N], an_v[:, i, q, :], ACT.Copy,
                                                  scale=factor(1 - par, SO, i, q))
                        last.then_inc(act_ahi, 1)
                if cur:
                    for j in range(4):
                        act.wait_ge(pe_m, 4 * t + j + 1)
                        act.activation(pr[:, 512 * j:512 * (j + 1)], g_bank(j), ACT.Exp, scale=SCALE)\
                            .then_inc(act_exp, 1)
                if nxt:
                    act.wait_ge(pool_par, t + 2)
                    if prev:
                        act.wait_ge(pe_o, 4 * t)
                    elif cur:
                        act.wait_ge(pe_q, 4 * (t + 1))
                    for i in range(KT):
                        act.wait_ge(pe_t, 4 * (t + 1) + i + 1)
                        for q in range(Q):
                            last = act.activation(hi[:, i, q * N:(q + 1) * N], w_bank(i)[:, q * N:(q + 1) * N],
                                                  ACT.Copy, scale=factor(1 - par, SK, i, q))
                        last.then_inc(act_hi, 1)
                        if prev:
                            act.wait_ge(dve_x1, 4 * (t - 1) + i + 1)
                        act.activation(xtb_v[:, 1 - par, i].rearrange("p q n -> p (q n)"), w_bank(i), ACT.Identity,
                                       bias=bias[:, 1, i:i + 1]).then_inc(act_xtb, 1)
                if cur:
                    if prev:
                        act.wait_ge(pe_pv, 4 * t)
                    for j in range(4):
                        act.wait_ge(pe_v, 4 * t + j + 1)
                        act.activation(vt[:, 512 * j:512 * (j + 1)], w_bank(j), ACT.Copy).then_inc(act_v, 1)
                if nxt:
                    if cur:
                        act.wait_ge(k_moved, 256 * (t + 1))
                    for m in range(4):
                        act.wait_ge(pe_q, 4 * (t + 1) + m + 1)
                        for q in range(Q):
                            last = act.activation(kn_v[:, m, q, :], w_bank(m)[:, q * N:(q + 1) * N], ACT.Identity,
                                                  bias=bias[:, 0, m:m + 1], scale=factor(1 - par, DK, m, q))
                        last.then_inc(act_k, 1)
                if cur:
                    if prev:
                        act.wait_ge(a_moved, 256 * t)
                    for j in range(4):
                        act.wait_ge(pe_pv, 4 * t + j + 1)
                        act.activation(aq_v[:, :, :, 4 * j:4 * (j + 1)],
                                       g_bank(j).rearrange("p (g c e) -> p e c g", g=4, c=4), ACT.Copy)\
                            .then_inc(act_aq, 1)
                if prev:
                    act.wait_ge(pe_z, t)
                    act.wait_ge(pool_ub, t)
                    act.activation(zt[:, :], w_bank(0)[:, 0:N], ACT.Identity,
                                   bias=ub_st[:, 1 - par:2 - par]).then_inc(act_z, 1)
                    for b in range(Q):
                        act.wait_ge(pe_y, 4 * (t - 1) + b + 1)
                        if b >= 2:
                            act.wait_ge(dve_out, 4 * (t - 1) + b - 1)
                        elif type(t) is not int or t >= 2:
                            act.wait_ge(dve_out, 4 * (t - 2) + b + 3)
                        act.activation(y2_v[:, b % 2, :], w_bank(1 + 2 * (b % 2)), ACT.Copy).then_inc(act_y, 1)

            steps(act, body)

        @block.vector
        def _(dve):
            pv = par[:, :, :].rearrange("p t (k f q) -> p k f t q", k=4, f=KT)
            dve.wait_ge(ld_small, 32)
            for w in range(2):
                dve.wait_ge(act_sty, w + 1)
                for f in range(KT):
                    last = dve.tensor_scalar(pv[:, (SK, SO)[w], f],
                                             w_bank(1 + w)[:, f * B:(f + 1) * B].rearrange("p (t q) -> p t q", q=Q),
                                             aff_b[:, w, f:f + 1], None, ALU.add)
                last.then_inc(dve_sty, 1)
            for w in range(2):
                for i in range(KT):
                    dve.wait_ge(act_wsq, 4 * w + i + 1)
                    dve.tensor_tensor(w_lo[w][:, i, :], (w_bank if w else g_bank)(i), w_hi[w][:, i, :].bitcast(f32),
                                      ALU.subtract).then_inc(dve_wlo, 1)
            for w in range(2):
                dve.wait_ge(pe_dem, w + 1)
                dve.tensor_scalar(dem[:, w, :], g_bank(w)[:, 0:KT * B], EPS, None, ALU.add).then_inc(dve_sum, 1)
            for w in range(2):
                dve.wait_ge(act_root, w + 1)
                dve.reciprocal(inv[:, w, :], root[:, w, :]).then_inc(dve_newton, 1)
                dve.wait_ge(dve_newton, 4 * w + 1)
                dve.tensor_tensor(root[:, w, :], inv[:, w, :], inv[:, w, :], ALU.mult).then_inc(dve_newton, 1)
                dve.wait_ge(dve_newton, 4 * w + 2)
                dve.tensor_tensor(root[:, w, :], root[:, w, :], dem[:, w, :], ALU.mult).then_inc(dve_newton, 1)
                dve.wait_ge(dve_newton, 4 * w + 3)
                dve.tensor_scalar(root[:, w, :], root[:, w, :], -0.5, 1.5, ALU.mult, ALU.add).then_inc(dve_newton, 1)
                dve.wait_ge(dve_newton, 4 * w + 4)
                for f in range(KT):
                    c = slice(f * B, (f + 1) * B)
                    last = dve.tensor_tensor(pv[:, (DK, DO)[w], f],
                                             inv[:, w, c].rearrange("p (t q) -> p t q", q=Q),
                                             root[:, w, c].rearrange("p (t q) -> p t q", q=Q), ALU.mult)
                last.then_inc(dve_dem, 1)
            dve.wait_ge(ld_v, 16 * (4 + 2 * Q))
            dve.wait_ge(pe_w, 8)
            for n in range(2):
                dve.memset(us[n][:, :, :, K:KP], 0.0).then_inc(dve_pad, 1)
            dve.wait_ge(dve_pad, 2)
            for it in range(KT):
                if it >= 2:
                    dve.wait_ge(st_u[it % 2], 16)
                for n in range(4):
                    ks = min(8, K - 8 * n)
                    dve.wait_ge(pe_u, 4 * it + n + 1)
                    dve.tensor_tensor(us[it % 2][:, :, :, 8 * n:8 * n + ks].rearrange("p t q k -> p (t q) k"),
                                      w_bank(n)[:, 0:ks * B].rearrange("p (k b) -> p b k", b=B),
                                      bdec[:, it, 8 * n:8 * n + ks].unsqueeze(1).to_broadcast([P, B, ks]),
                                      ALU.add).then_inc(dve_u, 1)

            def factor(par_, kind, i, q):
                n = (kind * KT + i) * Q + q
                return pst[:, par_, n:n + 1]

            def body(t, par, nxt, cur, prev):
                if prev:
                    for i in range(KT):
                        dve.wait_ge(act_ahi, 4 * (t - 1) + i + 1)
                        for q in range(Q):
                            c = slice(q * N, (q + 1) * N)
                            last = dve.scalar_tensor_tensor(out=lo[:, i, c], in0=an_v[:, i, q, :],
                                                            scalar=factor(1 - par, SO, i, q),
                                                            in1=hi[:, i, c].bitcast(f32),
                                                            op0=ALU.mult, op1=ALU.subtract)
                        last.then_inc(dve_alo, 1)
                if cur:
                    if prev:
                        dve.wait_ge(pool_md, 4 * t)
                    for j in range(4):
                        dve.wait_ge(pe_s, 4 * t + j + 1)
                        dve.tensor_reduce(rmax[:, 16 * j:16 * (j + 1)],
                                          g_bank(j).rearrange("p (a e) -> p a e", e=32), axis=AX.X, op=ALU.max)\
                            .then_inc(dve_max, 1)
                if prev:
                    if type(t) is not int or t >= 2:
                        dve.wait_ge(pe_x, 4 * (t - 1))
                    for m in range(4):
                        dve.wait_ge(pe_o, 4 * (t - 1) + m + 1)
                        dve.wait_ge(act_xtb, 4 * (t - 1) + m + 1)
                        for q in range(Q):
                            last = dve.scalar_tensor_tensor(out=x1_v[:, m, q, :], in0=w_bank(m)[:, q * N:(q + 1) * N],
                                                            scalar=factor(1 - par, DO, m, q),
                                                            in1=xtb_v[:, 1 - par, m, q, :],
                                                            op0=ALU.mult, op1=ALU.add)
                        last.then_inc(dve_x1, 1)
                if nxt:
                    dve.wait_ge(pool_par, t + 2)
                    for i in range(KT):
                        dve.wait_ge(act_xtb, 4 * (t + 1) + i + 1)
                        for q in range(Q):
                            c = slice(q * N, (q + 1) * N)
                            last = dve.scalar_tensor_tensor(out=lo[:, i, c], in0=w_bank(i)[:, c],
                                                            scalar=factor(1 - par, SK, i, q),
                                                            in1=hi[:, i, c].bitcast(f32),
                                                            op0=ALU.mult, op1=ALU.subtract)
                        last.then_inc(dve_lo, 1)
                if cur:
                    for j in range(4):
                        dve.wait_ge(pe_d, 4 * t + j + 1)
                        dve.reciprocal(g_bank(j), g_bank(j)).then_inc(dve_rec, 1)
                    for j in range(4):
                        dve.wait_ge(dve_rec, 4 * t + j + 1)
                        c = slice(512 * j, 512 * (j + 1))
                        dve.tensor_tensor(pr[:, c], pr[:, c], g_bank(j), ALU.mult).then_inc(dve_div, 1)
                    dve.wait_ge(dve_div, 4 * (t + 1))
                    for q in range(Q):
                        r = slice(32 * q, 32 * (q + 1))
                        last = dve.tensor_copy(bd[r, q, :], pr[r, :])
                    last.then_inc(dve_bp, 1)
                if nxt:
                    dve.wait_ge(k_moved, 256 * (t + 2))
                    if cur:
                        dve.wait_ge(pe_v, 4 * (t + 1))
                    dve.tensor_copy(kp[:, :, :, :].rearrange("p c e g -> p e c g"), kq_v).then_inc(dve_kp, 1)
                    if cur:
                        dve.wait_ge(pe_pv, 4 * (t + 1))
                    else:
                        dve.wait_ge(zeroed, 1)
                    for q in range(Q):
                        r = slice(32 * q, 32 * (q + 1))
                        last = dve.tensor_copy(bd[r, q, :], kq[r, :])
                    last.then_inc(dve_bs, 1)
                if prev:
                    for b in range(Q):
                        dve.wait_ge(pe_x, 4 * (t - 1) + b + 1)
                        dve.wait_ge(act_y, 4 * (t - 1) + b + 1)
                        if b >= 2:
                            dve.wait_ge(stored[b % 2], 16 * (2 * (t - 1) + 1))
                        elif type(t) is not int or t >= 2:
                            dve.wait_ge(stored[b % 2], 16 * 2 * (t - 1))
                        dve.tensor_tensor(ob_v[:, b % 2, :], w_bank((2, 0)[b % 2]), y2_v[:, b % 2, :], ALU.add)\
                            .then_inc(dve_out, 1)

            steps(dve, body)


_INS = ['x', 'cond_512', 'L0_cond_k_aff_w', 'L0_cond_k_aff_b', 'L0_cond_k_w', 'L0_cond_k_b', 'L0_cond_o_aff_w',
        'L0_cond_o_aff_b', 'L0_cond_o_w', 'L0_cond_o_b', 'L1_cond_W_dec', 'L1_cond_b_dec', 'L1_cond_V']


def kernel(**inputs):
    import numpy as _np
    import concourse.bacc as _bacc
    from concourse import mybir as _mybir
    from concourse.bass_utils import run_bass_kernel_spmd as _run

    nc = _bacc.Bacc("TRN2", target_bir_lowering=False, num_devices=1)
    arrays, args = {}, []
    for name in _INS:
        a = _np.ascontiguousarray(inputs[name])
        arrays[f"in_{name}_dram"] = a
        args.append(nc.dram_tensor(f"in_{name}_dram", a.shape, _mybir.dt.from_np(a.dtype), kind="ExternalInput").ap())
    shape = inputs['x'].shape
    args.append(nc.dram_tensor("out_0_dram", shape, _mybir.dt.float32, kind="ExternalOutput").ap())
    cond_resid_kernel(nc, *args)
    r = _run(nc, [arrays], core_ids=[0])
    return r.results[0]["out_0_dram"]
```

```python
import concourse.bass as bass
from concourse import mybir
from contextlib import ExitStack


def cond_resid_kernel(
    nc: bass.Bass,
    x: bass.AP,
    cond: bass.AP,
    k_aff_w: bass.AP,
    k_aff_b: bass.AP,
    k_w: bass.AP,
    k_b: bass.AP,
    o_aff_w: bass.AP,
    o_aff_b: bass.AP,
    o_w: bass.AP,
    o_b: bass.AP,
    W_dec: bass.AP,
    b_dec: bass.AP,
    V: bass.AP,
    out: bass.AP,
):
    f32 = mybir.dt.float32
    f32r = mybir.dt.float32r
    bf16 = mybir.dt.bfloat16
    ALU = mybir.AluOpType
    ACT = mybir.ActivationFunctionType
    AX = mybir.AxisListType

    B, N, F = x.shape
    S = cond.shape[1]
    K = V.shape[0]
    H = 16
    D = F // H
    P = 128
    Q = 4
    T = B // Q
    KT = F // P
    ST = S // P
    TOK = Q * N
    GG = N // 8
    E = 2 * H
    DQ = 2
    KP = 32
    SCALE = float(D) ** -0.5
    EPS = 1e-8
    BIG = 1e30
    COLS = H * N
    SK, DK, SO, DO = range(4)
    NPAR = 4 * KT * Q

    ctx = ExitStack()
    with ctx:
        def sb(name, shape, dt=f32):
            return ctx.enter_context(nc.sbuf_tensor(name, shape, dt))

        def sem(name):
            return ctx.enter_context(nc.semaphore(name))

        arena = sb("arena", [P, 8192 + 6 * 2048 + 2048 + 3 * 2048])
        at = [0]

        def cut(n):
            at[0] += n
            return arena[:, at[0] - n:at[0]]

        blockdiag = cut(8192)
        x1t = cut(2048)
        aq = cut(2048)
        an = cut(2048)
        pr = cut(2048)
        vt = cut(2048)
        yb = cut(2048)
        xtok = cut(2048)
        xtb = cut(6144)

        bd = blockdiag.rearrange("p (c m) -> p c m", c=Q)
        bd_scores = blockdiag.rearrange("p (q c e g) -> p q c e g", q=Q, c=4, e=E)
        bd_probs = blockdiag.rearrange("p (c g q e) -> p c g q e", c=Q, g=GG, q=Q)
        kn_v = x1t.rearrange("p (m q n) -> p m q n", m=KT, q=Q)
        kq_v = aq.rearrange("p (e c g) -> p e c g", e=E, c=4)
        kq_s = aq.rearrange("p (m k n) -> p m k n", m=KT, k=4)
        v_v = vt.rearrange("p (g q d) -> p g q d", g=GG, q=Q)
        aq_v = aq.rearrange("p (e c g) -> p e c g", e=E, c=4)
        aq_s = aq.rearrange("p (m k n) -> p m k n", m=KT, k=4)
        an_v = an.rearrange("p (m q n) -> p m q n", m=KT, q=Q)
        x1_v = x1t.rearrange("p (m q n) -> p m q n", m=KT, q=Q)
        yb_v = yb.rearrange("p (q f) -> p q f", q=Q)
        xtok_v = xtok.rearrange("p (q f) -> p q f", q=Q)
        xtb_v = xtb.rearrange("p (s m q n) -> p s m q n", s=3, m=KT, q=Q)

        hi = sb("hi", [P, KT, TOK], f32r)
        lo = sb("lo", [P, KT, TOK], f32r)
        w_hi = [sb(f"w_hi{n}", [P, KT, F], f32r) for n in range(2)]
        w_lo = [sb(f"w_lo{n}", [P, KT, F], f32r) for n in range(2)]
        md = sb("md", [P, GG * Q, 32], f32r)
        rmax = sb("rmax", [P, GG * Q])
        par = sb("par", [P, T, NPAR])
        pst = sb("pst", [P, 3, NPAR])
        ubias = sb("ubias", [P, T])
        ub_st = sb("ub_st", [P, 3])
        ust = sb("ust", [P, KT, Q, KP])
        z_hi = sb("z_hi", [P, N], f32r)
        z_lo = sb("z_lo", [P, N], f32r)
        v_hi = sb("v_hi", [P, Q, F], f32r)
        v_lo = sb("v_lo", [P, Q, F], f32r)
        kp = sb("kp", [P, 4, E, GG])
        ident = sb("ident", [P, P])
        eye32 = sb("eye32", [P, 32])
        ones_bd = sb("ones_bd", [P, P])
        neg_bd = sb("neg_bd", [P, P], f32r)
        mask_l = sb("mask_l", [2, P], bf16)
        mask_r = sb("mask_r", [2, TOK], bf16)
        aff_b = sb("aff_b", [P, 2, KT])
        bias = sb("bias", [P, 2, KT])
        bdec = sb("bdec", [P, KT, K])
        wlast = sb("wlast", [P, ST, KP])
        blast = sb("blast", [P, 1])
        ct = sb("ct", [P, ST, B])
        sty2 = xtb[:, 4096:4096 + 2 * KT * B].rearrange("p (w f b) -> p w f b", w=2, f=KT)
        cond_sb = xtb[0:B, 4608:4608 + S]

        spare = kp[:, :, :, :].rearrange("p c e g -> p (c e g)")
        dem, root, inv = (spare[:, n * 2 * KT * B:(n + 1) * 2 * KT * B].rearrange("p (w n) -> p w n", w=2)
                          for n in range(3))
        v_rep = spare[:, 3 * 2 * KT * B:3 * 2 * KT * B + F]
        aff_in = xtb[:, 0:2048].rearrange("p (w t s) -> p w t s", w=2, t=KT)
        aff_t = xtb[:, 2048:4096].rearrange("p (w s f) -> p w s f", w=2, s=ST)
        w_in = [blockdiag[:, 2048 * n:2048 * (n + 1)].rearrange("p (t i) -> p t i", t=KT) for n in (2, 3)]
        w_sq = [blockdiag[:, 2048 * n:2048 * (n + 1)].rearrange("p (t o) -> p t o", t=KT) for n in (0, 1)]
        CI = 16
        CH = P // CI
        CC = CI * K
        wc = [arena[:, 8192 + 4 * CC * n:8192 + 4 * CC * (n + 1)].rearrange("p (m h c) -> p m h c", m=ST, h=2)
              for n in range(4)]
        u_raw = [blockdiag[:, P * K * n:P * K * (n + 1)] for n in range(2)]
        us = [arena[:, 16384 + 2048 * n:16384 + 2048 * (n + 1)].rearrange("p (t q k) -> p t q k", t=T, q=Q)
              for n in range(2)]

        u_dram = nc.dram_tensor("u_scratch", [T, P, KT, Q, KP], f32)

        Gp = ctx.enter_context(nc.psum_tensor("Gp", [P, 4, TOK], f32))
        Wp = ctx.enter_context(nc.psum_tensor("Wp", [P, 4, TOK], f32))

        def g_bank(j):
            return Gp[:, j, :]

        def w_bank(j):
            return Wp[:, j, :]

        ld_cond, ld_aff, ld_w, ld_small, ld_v = (sem(n) for n in ("ld_cond", "ld_aff", "ld_w", "ld_small", "ld_v"))
        ld_wc = [sem(f"ld_wc{n}") for n in range(4)]
        st_u = [sem("st_u0"), sem("st_u1")]
        cst = sem("cst")
        cst_part = sem("cst_part")
        zeroed = sem("zeroed")
        pe_ct, act_ct = sem("pe_ct"), sem("act_ct")
        pe_aff, act_aff = sem("pe_aff"), sem("act_aff")
        pe_sty, dve_sty, act_sty = sem("pe_sty"), sem("dve_sty"), sem("act_sty")
        pe_w, act_whi, act_wsq, dve_wlo = sem("pe_w"), sem("act_whi"), sem("act_wsq"), sem("dve_wlo")
        pe_dem, dve_dem = sem("pe_dem"), sem("dve_dem")
        dve_sum, act_root, dve_newton = sem("dve_sum"), sem("act_root"), sem("dve_newton")
        act_ln, act_rec, dve_zlo = sem("act_ln"), sem("act_rec"), sem("dve_zlo")
        act_vhi, dve_vlo = sem("act_vhi"), sem("dve_vlo")
        pe_ul, act_ul = sem("pe_ul"), sem("act_ul")
        pe_u, act_u, pe_ut, dve_u, dve_pad = (sem(n) for n in ("pe_u", "act_u", "pe_ut", "dve_u", "dve_pad"))
        x_in = sem("x_in")
        u_in = sem("u_in")
        k_moved, a_moved = sem("k_moved"), sem("a_moved")
        stored = [sem(f"stored{b}") for b in range(Q)]
        pe_t, pe_q, pe_s, pe_m, pe_d, pe_v, pe_pv, pe_o, pe_z, pe_y, pe_x = (
            sem(n) for n in ("pe_t", "pe_q", "pe_s", "pe_m", "pe_d", "pe_v", "pe_pv", "pe_o", "pe_z", "pe_y", "pe_x"))
        pe_hilo = sem("pe_hilo")
        act_hi, act_xtb, act_k, act_v, act_exp, act_aq, act_ahi, act_z, act_y, act_bp = (
            sem(n) for n in ("act_hi", "act_xtb", "act_k", "act_v", "act_exp", "act_aq", "act_ahi", "act_z", "act_y", "act_bp"))
        dve_lo, dve_max, dve_div, dve_bp, dve_bs, dve_alo, dve_x1, dve_out, dve_kp = (
            sem(n) for n in ("dve_lo", "dve_max", "dve_div", "dve_bp", "dve_bs", "dve_alo", "dve_x1", "dve_out", "dve_kp"))
        pool_md, pool_par, pool_ub = sem("pool_md"), sem("pool_par"), sem("pool_ub")

        def steps(eng, body):
            for t in (-1, 0, 1):
                body(t, t % 3, True, t >= 0, t >= 1)
            with eng.Fori(0, (T - 4) // 3) as triple:
                for n in range(2, 5):
                    body(3 * triple + n, n % 3, True, True, True)
            for t in (T - 2, T - 1, T):
                body(t, t % 3, t < T - 1, t < T, True)

        def later(t):
            return type(t) is not int or t >= 2

        block = ctx.enter_context(nc.Block())

        @block.sync
        def _(sp):
            sp.dma_start(cond_sb, cond[:, :]).then_inc(ld_cond, 16)
            for w, a in enumerate((k_aff_w, o_aff_w)):
                sp.dma_start(aff_in[:, w], a.rearrange("(t p) s -> p t s", p=P)).then_inc(ld_aff, 16)
            for w, a in enumerate((k_aff_b, o_aff_b)):
                sp.dma_start(aff_b[:, w, :], a.rearrange("(t p) -> p t", p=P),
                             allow_slow_non_contiguous=True).then_inc(ld_small, 16)
            for w, a in enumerate((k_w, o_w)):
                sp.dma_start(w_in[w], a.rearrange("(t p) i -> p t i", p=P)).then_inc(ld_w, 16)
            sp.dma_start(xtok_v, x[0:Q].rearrange("q n f -> n q f")).then_inc(x_in, 16)
            for n in range(2 * CH):
                pair, ch = n // CH, n % CH
                if n >= 4:
                    sp.wait_ge(pe_u, n - 3)
                src = W_dec[:, 2 * pair * P * K:2 * (pair + 1) * P * K].rearrange("(m p) (h c) -> p m h c", p=P, h=2)
                for m in range(ST):
                    sp.dma_start(wc[n % 4][:, m], src[:, m, :, ch * CC:(ch + 1) * CC]).then_inc(ld_wc[n % 4], 16)
            for it in range(KT):
                sp.wait_ge(dve_u, 16 * (it // 2 + 1))
                sp.dma_start(u_dram[:, :, it, :, :].rearrange("t p q k -> p t q k"), us[it % 2])\
                  .then_inc(st_u[it % 2], 16)
            for n in range(2):
                sp.wait_ge(st_u[n], 32)

            def body(t, r, nxt, cur, prev):
                static = type(t) is int
                at_once = (lambda v: v) if static else sp.to_reg
                t_of_next, k_of_next = at_once(4 * (t + 2)), at_once(4 * (t + 2))
                aq_made, tiles_before = at_once(4 * (t + 1)), at_once(4 * t)
                a_moves, steps_before = at_once(256 * t), at_once(t)
                outs = [at_once(4 * (t - 1) + b + 1) for b in range(Q)]
                if nxt:
                    if not static or t < T - 2:
                        sp.wait_ge(pe_t, t_of_next)
                        sp.dma_start(xtok_v, x[bass.ds(Q * (t + 2), Q)].rearrange("q n f -> n q f")).then_inc(x_in, 16)
                    sp.wait_ge(act_k, k_of_next)
                    if prev:
                        sp.wait_ge(a_moved, a_moves)
                    for k in range(4):
                        for q in range(Q):
                            sp.dma_start(kq_s[D * q:D * (q + 1), :, k, :], kn_v[D * k:D * (k + 1), :, q, :])\
                              .then_inc(k_moved, 16)
                if cur:
                    sp.wait_ge(act_aq, aq_made)
                    if prev:
                        sp.wait_ge(act_ahi, tiles_before)
                        sp.wait_ge(dve_alo, tiles_before)
                    for k in range(4):
                        for q in range(Q):
                            sp.dma_start(an_v[D * k:D * (k + 1), :, q, :], aq_s[D * q:D * (q + 1), :, k, :])\
                              .then_inc(a_moved, 16)
                    if prev:
                        sp.wait_ge(pe_z, steps_before)
                    sp.dma_start(ust[:, :, :, :], u_dram[t]).then_inc(u_in, 16)
                if prev:
                    for b in range(Q):
                        sp.wait_ge(dve_out, outs[b])
                        sp.dma_start(out[Q * (t - 1) + b], yb_v[:, b, :]).then_inc(stored[b], 16)

            steps(sp, body)
            for b in range(Q):
                sp.wait_ge(stored[b], 16 * T)

        @block.gpsimd
        def _(pool):
            pool.memset(ident[:, :], 0.0).then_inc(cst_part, 1)
            pool.memset(ones_bd[:, :], 0.0).then_inc(cst_part, 1)
            pool.memset(neg_bd[:, :].bitcast(f32), 0.0).then_inc(cst_part, 1)
            pool.memset(mask_l[:, :], 0.0).then_inc(cst_part, 1)
            pool.memset(mask_r[:, :], -BIG).then_inc(cst_part, 1)
            pool.memset(wlast[:, :, :], 0.0).then_inc(cst_part, 1)
            pool.memset(blast[:, :], 0.0).then_inc(cst_part, 1)
            pool.memset(v_rep, 0.0).then_inc(cst_part, 1)
            pool.memset(v_hi[:, :, :].bitcast(f32), 0.0).then_inc(cst_part, 1)
            pool.memset(v_lo[:, :, :].bitcast(f32), 0.0).then_inc(cst_part, 1)
            pool.wait_ge(cst_part, 10)
            pool.affine_select(out=ident[:, :], in_=ident[:, :], compare_op=ALU.not_equal, fill=1.0, base=0,
                               pattern=[[-1, P]], channel_multiplier=1).then_inc(cst_part, 1)
            for m, fill in ((mask_l, 1.0), (mask_r, 0.0)):
                v = m[:, :].rearrange("k (a e) -> k a e", e=2)
                pool.affine_select(out=v, in_=v, compare_op=ALU.not_equal, fill=fill, base=0,
                                   pattern=[[0, v.shape[1]], [-1, 2]], channel_multiplier=1).then_inc(cst_part, 1)
            pool.wait_ge(cst_part, 13)
            for q in range(Q):
                r = slice(32 * q, 32 * (q + 1))
                pool.memset(ones_bd[r, r], 1.0).then_inc(cst, 1)
                pool.memset(neg_bd[r, r].bitcast(f32), -1.0).then_inc(cst, 1)
                pool.tensor_copy(eye32[r, :], ident[r, r]).then_inc(cst, 1)
            for w, a in enumerate((k_b, o_b)):
                pool.dma_start(bias[:, w, :], a.rearrange("(t p) -> p t", p=P),
                             allow_slow_non_contiguous=True).then_inc(ld_v, 16)
            pool.dma_start(wlast[:, :, 0:K], W_dec[:, F * K:(F + 1) * K].rearrange("(m p) k -> p m k", p=P))\
                .then_inc(ld_v, 16)
            pool.dma_start(bdec[:, :, :], b_dec[0:F * K].rearrange("(t p k) -> p t k", p=P, k=K)).then_inc(ld_v, 16)
            for q in range(Q):
                pool.dma_start(blast[KP * q:KP * q + K, :], b_dec[F * K:(F + 1) * K].rearrange("(k a) -> k a", a=1))\
                    .then_inc(ld_v, 16)
                pool.dma_start(v_rep[KP * q:KP * q + K, :], V[:, :]).then_inc(ld_v, 16)
            pool.wait_ge(pe_ut, 16)
            pool.memset(blockdiag, 0.0).then_inc(zeroed, 1)

            pool.wait_ge(dve_sty, 2)
            pool.wait_ge(dve_dem, 2)
            pool.wait_ge(act_ul, 1)

            def body(t, r, nxt, cur, prev):
                if nxt:
                    if later(t):
                        pool.wait_ge(dve_x1, 4 * (t - 1))
                    pool.tensor_copy(pst[:, (r + 1) % 3, :],
                                     par[:, bass.ds(t + 1, 1), :].rearrange("p a n -> p (a n)")).then_inc(pool_par, 1)
                if cur:
                    if later(t):
                        pool.wait_ge(dve_zlo, t - 1)
                    pool.tensor_copy(ub_st[:, r:r + 1], ubias[:, bass.ds(t, 1)]).then_inc(pool_ub, 1)
                    for j in range(4):
                        pool.wait_ge(dve_max, 4 * t + j + 1)
                        if prev:
                            pool.wait_ge(pe_m, 4 * (t - 1) + j + 1)
                        c = slice(16 * j, 16 * (j + 1))
                        pool.tensor_tensor(md[:, c, :], rmax[:, c].unsqueeze(2).to_broadcast([P, 16, 32]),
                                           eye32[:, :].unsqueeze(1).to_broadcast([P, 16, 32]), ALU.mult)\
                            .then_inc(pool_md, 1)

            steps(pool, body)

        @block.tensor
        def _(pe):
            pe.wait_ge(cst_part, 13)
            pe.wait_ge(cst, 12)
            pe.wait_ge(ld_cond, 16)
            for s in range(ST):
                last = pe.transpose(w_bank(0)[:, s * B:(s + 1) * B], cond_sb[:, s * P:(s + 1) * P], ident[0:B, 0:B])
            last.then_inc(pe_ct, 1)
            pe.wait_ge(ld_aff, 32)
            for w in range(2):
                for s in range(ST):
                    for f in range(KT):
                        last = pe.transpose(g_bank(2 * w + s)[:, f * P:(f + 1) * P],
                                            aff_in[:, w, f, s * P:(s + 1) * P], ident[:, :])
                    last.then_inc(pe_aff, 1)
            pe.wait_ge(act_ct, 1)
            pe.wait_ge(act_aff, 4)
            for w in range(2):
                for f in range(KT):
                    for s in range(ST):
                        last = pe.matmul(w_bank(1 + w)[:, f * B:(f + 1) * B], aff_t[:, w, s, f * P:(f + 1) * P],
                                         ct[:, s, :], start=(s == 0), stop=(s == ST - 1))
                last.then_inc(pe_sty, 1)
            pe.wait_ge(ld_w, 32)
            for w in range(2):
                for i in range(KT):
                    if w == 1 and i in (1, 2):
                        pe.wait_ge(dve_sty, 2)
                        pe.wait_ge(act_sty, 2)
                    for o in range(KT):
                        last = pe.transpose((w_bank if w else g_bank)(i)[:, o * P:(o + 1) * P],
                                            w_in[w][:, o, i * P:(i + 1) * P], ident[:, :])
                    last.then_inc(pe_w, 1)
            pe.wait_ge(act_sty, 2)
            for w in range(2):
                pe.wait_ge(act_wsq, 4 * (w + 1))
                pe.wait_ge(dve_wlo, 4)
                pe.wait_ge(act_whi, 4)
                for o in range(KT):
                    for i in range(KT):
                        last = pe.matmul(g_bank(w)[:, o * B:(o + 1) * B], w_sq[w][:, i, o * P:(o + 1) * P],
                                         sty2[:, w, i, :], start=(i == 0), stop=(i == KT - 1))
                last.then_inc(pe_dem, 1)
            pe.wait_ge(dve_wlo, 8)
            pe.wait_ge(act_whi, 8)
            pe.wait_ge(act_wsq, 8)
            pe.wait_ge(dve_sum, 2)
            for pair in range(2):
                for ch in range(CH):
                    n = CH * pair + ch
                    pe.wait_ge(ld_wc[n % 4], 32 * (n // 4 + 1))
                    if n >= 4:
                        pe.wait_ge(act_u, n - 3)
                    for m in range(ST):
                        for h in range(2):
                            last = pe.matmul(w_bank(n % 4)[B * h:B * (h + 1), 0:CC], ct[:, m, :], wc[n % 4][:, m, h, :],
                                             start=(m == 0), stop=(m == ST - 1))
                    last.then_inc(pe_u, 1)
                pe.wait_ge(act_u, CH * (pair + 1))
                for n in range(8):
                    if pair or n >= 4:
                        pe.wait_ge(dve_u, 2 * (8 * pair + n - 3))
                    for k in range(4 * n, min(4 * n + 4, K)):
                        last = pe.transpose(g_bank(n % 4)[:, (k % 4) * P:(k % 4 + 1) * P],
                                            u_raw[pair].rearrange("p (i k) -> p i k", k=K)[:, :, k], ident[:, :])
                    last.then_inc(pe_ut, 1)
            pe.wait_ge(ld_v, 16 * (4 + 2 * Q))
            pe.wait_ge(dve_u, 2 * 15)
            for q in range(Q):
                for s in range(ST):
                    last = pe.matmul(g_bank(2)[KP * q:KP * (q + 1), 0:T], wlast[:, s, :],
                                     ct[:, s, :].rearrange("p (t q) -> p t q", q=Q)[:, :, q],
                                     start=(s == 0), stop=(s == ST - 1))
            last.then_inc(pe_ul, 1)

            def project(w, tiles, done, bank_free, part_ready, part_used=None):
                for i in range(KT):
                    part_ready(i)
                    for m in tiles:
                        if i == 0:
                            bank_free(m)
                        for n, (a, b) in enumerate(((w_hi, hi), (w_hi, lo), (w_lo, hi))):
                            last = pe.matmul(w_bank(m), a[w][:, i, m * P:(m + 1) * P], b[:, i, :],
                                             start=(i == 0 and n == 0), stop=(i == KT - 1 and n == 2))
                        if i == KT - 1:
                            last.then_inc(done, 1)
                    if part_used is not None and i < KT - 1:
                        last.then_inc(part_used, 1)

            def body(t, r, nxt, cur, prev):
                def second_layer_left(bank):
                    pe.wait_ge(act_y, 4 * (t - 2) + bank + 1)

                if nxt:
                    pe.wait_ge(x_in, 16 * (t + 2))
                    for i in range(KT):
                        if later(t):
                            second_layer_left(i)
                        elif cur:
                            pe.wait_ge(act_k, 4 * t + i + 1)
                        else:
                            pe.wait_ge(act_u, 2 * CH)
                        for q in range(Q):
                            last = pe.transpose(w_bank(i)[:, q * N:(q + 1) * N], xtok_v[:, q, i * P:(i + 1) * P],
                                                ident[:, :])
                        last.then_inc(pe_t, 1)
                if cur:
                    pe.wait_ge(dve_kp, t + 1)
                    pe.wait_ge(dve_bs, t + 1)
                    for j in range(4):
                        if later(t):
                            pe.wait_ge(dve_out, 4 * (t - 2) + j + 1)
                        elif prev:
                            pe.wait_ge(act_aq, 4 * (t - 1) + j + 1)
                        pe.matmul(g_bank(j), mask_l[:, :], mask_r[:, :], start=True, stop=False,
                                  skip_group_check=True)
                        for g in range(4 * j, 4 * j + 4):
                            for c in range(4):
                                last = pe.matmul(g_bank(j)[32 * c:32 * (c + 1), (g % 4) * P:(g % 4 + 1) * P],
                                                 kp[:, c, :, g], bd_scores[:, :, c, :, g],
                                                 start=False, stop=False, skip_group_check=True)
                        last.then_inc(pe_s, 1)
                    for j in range(4):
                        if nxt:
                            pe.wait_ge(act_xtb, 4 * (t + 1) + j + 1)
                            pe.wait_ge(dve_lo, 4 * (t + 1) + j + 1)
                        else:
                            second_layer_left(j)
                        for g in range(4 * j, 4 * j + 4):
                            last = pe.transpose(w_bank(j)[:, (g % 4) * P:(g % 4 + 1) * P],
                                                kp[:, :, :, g].rearrange("p c e -> p (c e)"), ident[:, :])
                        last.then_inc(pe_v, 1)

                def k_projection(*tiles):
                    def bank_free(m):
                        if cur:
                            pe.wait_ge(act_v, 4 * t + m + 1)
                        else:
                            pe.wait_ge(act_xtb, 4 * (t + 1) + m + 1)
                            pe.wait_ge(dve_lo, 4 * (t + 1) + m + 1)

                    def part_ready(i):
                        if 0 in tiles:
                            pe.wait_ge(act_hi, 4 * (t + 1) + i + 1)
                            pe.wait_ge(dve_lo, 4 * (t + 1) + i + 1)

                    project(0, tiles, pe_q, bank_free, part_ready, pe_hilo if 3 in tiles else None)

                if nxt:
                    k_projection(0)
                    k_projection(1)
                if cur:
                    for j in range(4):
                        pe.wait_ge(pool_md, 4 * t + j + 1)
                        pe.matmul(g_bank(j), neg_bd[:, :], md[:, 16 * j:16 * (j + 1), :].rearrange("p a e -> p (a e)"),
                                  start=False, stop=True, skip_group_check=True).then_inc(pe_m, 1)
                if nxt:
                    k_projection(2)
                    k_projection(3)
                if cur:
                    for j in range(4):
                        pe.wait_ge(act_exp, 4 * t + j + 1)
                        pe.matmul(g_bank(j), ones_bd[:, :], pr[:, 512 * j:512 * (j + 1)], start=True, stop=True)\
                            .then_inc(pe_d, 1)
                if prev:
                    def bank_free(m):
                        if nxt:
                            pe.wait_ge(act_k, 4 * (t + 1) + m + 1)
                        elif cur:
                            pe.wait_ge(act_v, 4 * t + m + 1)
                        else:
                            second_layer_left(m)

                    def part_ready(i):
                        pe.wait_ge(act_ahi, 4 * (t - 1) + i + 1)
                        pe.wait_ge(dve_alo, 4 * (t - 1) + i + 1)

                    for tiles in ((0, 1), (2,), (3,)):
                        project(1, tiles, pe_o, bank_free, part_ready)
                if cur:
                    pe.wait_ge(act_v, 4 * (t + 1))
                    for j in range(4):
                        if j % 2 == 0:
                            pe.wait_ge(dve_bp, 2 * t + j // 2 + 1)
                            pe.wait_ge(act_bp, 2 * t + j // 2 + 1)
                        for g in range(4 * j, 4 * j + 4):
                            for q in range(Q):
                                last = pe.matmul(g_bank(j)[32 * q:32 * (q + 1), (g % 4) * P:(g % 4 + 1) * P],
                                                 v_v[:, g, q, :], bd_probs[:, :, g, q, :], start=True, stop=True)
                        last.then_inc(pe_pv, 1)
                if prev:
                    pe.wait_ge(dve_x1, 4 * t)
                    pe.wait_ge(u_in, 16 * t)
                    for i in range(KT):
                        for q in range(Q):
                            last = pe.matmul(w_bank(0)[KP * q:KP * (q + 1), 0:N], ust[:, i, q, :],
                                             x1_v[:, i, q, :], start=(i == 0), stop=(i == KT - 1))
                    last.then_inc(pe_z, 1)
                    for b in range(Q):
                        if cur:
                            pe.wait_ge(act_aq, 4 * t + b + 1)
                        else:
                            pe.wait_ge(dve_out, 4 * (t - 2) + b + 1)
                        for i in range(KT):
                            last = pe.transpose(g_bank(b)[:, i * P:(i + 1) * P], x1_v[:, i, b, :], ident[:, :])
                        last.then_inc(pe_x, 1)
                    pe.wait_ge(dve_zlo, t)
                    for b in range(Q):
                        for n, (z, v) in enumerate(((z_hi, v_hi), (z_hi, v_lo), (z_lo, v_hi))):
                            last = pe.matmul(w_bank(b), z[:, :], v[:, b, :], start=(n == 0), stop=(n == 2))
                        last.then_inc(pe_y, 1)

            steps(pe, body)

        @block.scalar
        def _(act):
            act.wait_ge(pe_ct, 1)
            act.activation(ct[:, :, :].rearrange("p s b -> p (s b)"), w_bank(0)[:, 0:ST * B], ACT.Copy)\
                .then_inc(act_ct, 1)
            for n in range(4):
                act.wait_ge(pe_aff, n + 1)
                act.activation(aff_t[:, n // 2, n % 2, :], g_bank(n), ACT.Copy).then_inc(act_aff, 1)
            act.wait_ge(ld_small, 32)
            for w in range(2):
                act.wait_ge(pe_sty, w + 1)
                for f in range(KT):
                    last = act.activation(sty2[:, w, f, :], w_bank(1 + w)[:, f * B:(f + 1) * B], ACT.Square,
                                          bias=aff_b[:, w, f:f + 1])
                last.then_inc(act_sty, 1)
            for w in range(2):
                for i in range(KT):
                    act.wait_ge(pe_w, 4 * w + i + 1)
                    bank = (w_bank if w else g_bank)(i)
                    act.activation(w_hi[w][:, i, :], bank, ACT.Copy).then_inc(act_whi, 1)
                    act.activation(w_sq[w][:, i, :], bank, ACT.Square).then_inc(act_wsq, 1)
            for w in range(2):
                act.wait_ge(dve_sum, w + 1)
                act.activation(root[:, w, :], dem[:, w, :], ACT.Sqrt).then_inc(act_root, 1)
            act.preload_act_table_set("natural_log_exp_and_others")
            act.wait_ge(pe_dem, 2)
            for n in range(2 * CH):
                pair, ch = n // CH, n % CH
                act.wait_ge(pe_u, n + 1)
                act.activation(u_raw[pair][:, ch * CC:(ch + 1) * CC], w_bank(n % 4)[:, 0:CC], ACT.Copy)\
                    .then_inc(act_u, 1)
            act.wait_ge(ld_v, 16 * (4 + 2 * Q))
            act.wait_ge(cst_part, 13)
            for q in range(Q):
                r = slice(KP * q, KP * (q + 1))
                act.activation(v_hi[r, q, :], v_rep[r, :], ACT.Copy).then_inc(act_vhi, 1)
            act.wait_ge(pe_ul, 1)
            act.wait_ge(ld_v, 16 * (4 + 2 * Q))
            act.activation(ubias[:, :], g_bank(2)[:, 0:T], ACT.Identity, bias=blast[:, :]).then_inc(act_ul, 1)

            def factor(r, kind, i, q):
                n = (kind * KT + i) * Q + q
                return pst[:, r, n:n + 1]

            def body(t, r, nxt, cur, prev):
                if nxt:
                    act.wait_ge(pool_par, t + 2)
                    if later(t):
                        act.wait_ge(pe_o, 4 * (t - 1))
                        act.wait_ge(dve_x1, 4 * (t - 1))
                    elif cur:
                        act.wait_ge(pe_q, 4 * (t + 1))
                    for i in range(KT):
                        act.wait_ge(pe_t, 4 * (t + 1) + i + 1)
                        for q in range(Q):
                            last = act.activation(hi[:, i, q * N:(q + 1) * N], w_bank(i)[:, q * N:(q + 1) * N],
                                                  ACT.Copy, scale=factor((r + 1) % 3, SK, i, q))
                        last.then_inc(act_hi, 1)
                        act.activation(xtb_v[:, (r + 1) % 3, i].rearrange("p q n -> p (q n)"), w_bank(i), ACT.Identity,
                                       bias=bias[:, 1, i:i + 1]).then_inc(act_xtb, 1)
                if cur:
                    if prev:
                        act.wait_ge(pe_pv, 4 * t)
                    for j in range(4):
                        act.wait_ge(pe_v, 4 * t + j + 1)
                        act.activation(vt[:, 512 * j:512 * (j + 1)], w_bank(j), ACT.Copy).then_inc(act_v, 1)

                def k_out(m):
                    act.wait_ge(pe_q, 4 * (t + 1) + m + 1)
                    for q in range(Q):
                        last = act.activation(kn_v[:, m, q, :], w_bank(m)[:, q * N:(q + 1) * N], ACT.Identity,
                                              bias=bias[:, 0, m:m + 1], scale=factor((r + 1) % 3, DK, m, q))
                    last.then_inc(act_k, 1)

                if nxt:
                    if cur:
                        act.wait_ge(k_moved, 256 * (t + 1))
                    if later(t):
                        act.wait_ge(pe_x, 4 * (t - 1))
                    k_out(0)
                    k_out(1)
                if cur:
                    if prev:
                        act.wait_ge(dve_bp, 2 * t)
                        act.wait_ge(act_bp, 2 * t)
                    for j in range(4):
                        act.wait_ge(pe_m, 4 * t + j + 1)
                        act.activation(pr[:, 512 * j:512 * (j + 1)], g_bank(j), ACT.Exp, scale=SCALE)\
                            .then_inc(act_exp, 1)

                def attended_hi(i):
                    if i == 0:
                        act.wait_ge(a_moved, 256 * t)
                    if not nxt:
                        act.wait_ge(pe_o, 4 * (t - 1))
                    elif i < KT - 1:
                        act.wait_ge(pe_hilo, 3 * (t + 1) + i + 1)
                    for q in range(Q):
                        last = act.activation(hi[:, i, q * N:(q + 1) * N], an_v[:, i, q, :], ACT.Copy,
                                              scale=factor((r + 2) % 3, SO, i, q))
                    last.then_inc(act_ahi, 1)

                if nxt:
                    k_out(2)
                if prev:
                    attended_hi(0)
                if nxt:
                    k_out(3)
                if prev:
                    for i in range(1, KT):
                        attended_hi(i)
                if cur:
                    for h in range(2):
                        for j in (2 * h, 2 * h + 1):
                            act.wait_ge(pe_d, 4 * t + j + 1)
                            act.activation(g_bank(j), g_bank(j), ACT.Ln).then_inc(act_ln, 1)
                        for j in (2 * h, 2 * h + 1):
                            act.wait_ge(act_ln, 4 * t + j + 1)
                            act.activation(g_bank(j), g_bank(j), ACT.Exp, scale=-1.0).then_inc(act_rec, 1)
                    for h in range(2):
                        act.wait_ge(dve_div, 4 * t + 2 * h + 2)
                        c = slice(1024 * h, 1024 * (h + 1))
                        for q in range(DQ, Q):
                            p = slice(32 * q, 32 * (q + 1))
                            last = act.activation(bd[p, q, c], pr[p, c], ACT.Copy)
                        last.then_inc(act_bp, 1)
                    if nxt:
                        act.wait_ge(dve_kp, t + 2)
                    if prev:
                        act.wait_ge(a_moved, 256 * t)
                    for j in range(4):
                        act.wait_ge(pe_pv, 4 * t + j + 1)
                        act.activation(aq_v[:, :, :, 4 * j:4 * (j + 1)],
                                       g_bank(j).rearrange("p (g c e) -> p e c g", g=4, c=4), ACT.Copy)\
                            .then_inc(act_aq, 1)
                if prev:
                    act.wait_ge(pe_z, t)
                    act.wait_ge(pool_ub, t)
                    if later(t):
                        act.wait_ge(pe_y, 4 * (t - 1))
                    act.activation(z_hi[:, :], w_bank(0)[:, 0:N], ACT.Identity,
                                   bias=ub_st[:, (r + 2) % 3:(r + 2) % 3 + 1]).then_inc(act_z, 1)
                    for b in range(Q):
                        act.wait_ge(pe_y, 4 * (t - 1) + b + 1)
                        if later(t):
                            act.wait_ge(stored[b], 16 * (t - 1))
                        act.activation(yb_v[:, b, :], w_bank(b), ACT.Copy).then_inc(act_y, 1)

            steps(act, body)

        @block.vector
        def _(dve):
            pv = par[:, :, :].rearrange("p t (k f q) -> p k f t q", k=4, f=KT)
            dve.wait_ge(ld_small, 32)
            for w in range(2):
                dve.wait_ge(act_sty, w + 1)
                for f in range(KT):
                    last = dve.tensor_scalar(pv[:, (SK, SO)[w], f],
                                             w_bank(1 + w)[:, f * B:(f + 1) * B].rearrange("p (t q) -> p t q", q=Q),
                                             aff_b[:, w, f:f + 1], None, ALU.add)
                last.then_inc(dve_sty, 1)
            for w in range(2):
                for i in range(KT):
                    dve.wait_ge(act_wsq, 4 * w + i + 1)
                    dve.tensor_tensor(w_lo[w][:, i, :], (w_bank if w else g_bank)(i), w_hi[w][:, i, :].bitcast(f32),
                                      ALU.subtract).then_inc(dve_wlo, 1)
            for w in range(2):
                dve.wait_ge(pe_dem, w + 1)
                dve.tensor_scalar(dem[:, w, :], g_bank(w)[:, 0:KT * B], EPS, None, ALU.add).then_inc(dve_sum, 1)
            for w in range(2):
                dve.wait_ge(act_root, w + 1)
                dve.reciprocal(inv[:, w, :], root[:, w, :]).then_inc(dve_newton, 1)
                dve.wait_ge(dve_newton, 4 * w + 1)
                dve.tensor_tensor(root[:, w, :], inv[:, w, :], inv[:, w, :], ALU.mult).then_inc(dve_newton, 1)
                dve.wait_ge(dve_newton, 4 * w + 2)
                dve.tensor_tensor(root[:, w, :], root[:, w, :], dem[:, w, :], ALU.mult).then_inc(dve_newton, 1)
                dve.wait_ge(dve_newton, 4 * w + 3)
                dve.tensor_scalar(root[:, w, :], root[:, w, :], -0.5, 1.5, ALU.mult, ALU.add).then_inc(dve_newton, 1)
                dve.wait_ge(dve_newton, 4 * w + 4)
                for f in range(KT):
                    c = slice(f * B, (f + 1) * B)
                    last = dve.tensor_tensor(pv[:, (DK, DO)[w], f],
                                             inv[:, w, c].rearrange("p (t q) -> p t q", q=Q),
                                             root[:, w, c].rearrange("p (t q) -> p t q", q=Q), ALU.mult)
                last.then_inc(dve_dem, 1)
            dve.wait_ge(ld_v, 16 * (4 + 2 * Q))
            for n in range(2):
                dve.memset(us[n][:, :, :, K:KP], 0.0).then_inc(dve_pad, 1)
            dve.wait_ge(dve_pad, 2)
            for pair in range(2):
                for n in range(8):
                    ks = min(4, K - 4 * n)
                    dve.wait_ge(pe_ut, 8 * pair + n + 1)
                    for h in range(2):
                        if pair and not n:
                            dve.wait_ge(st_u[h], 16)
                        dve.tensor_tensor(us[h][:, :, :, 4 * n:4 * n + ks].rearrange("p t q k -> p (t q) k"),
                                          g_bank(n % 4)[:, 0:ks * P].rearrange("p (k h b) -> p h b k", h=2, b=B)[:, h],
                                          bdec[:, 2 * pair + h, 4 * n:4 * n + ks].unsqueeze(1).to_broadcast([P, B, ks]),
                                          ALU.add).then_inc(dve_u, 1)
            for q in range(Q):
                r = slice(KP * q, KP * (q + 1))
                dve.wait_ge(act_vhi, q + 1)
                dve.tensor_tensor(v_lo[r, q, :], v_rep[r, :], v_hi[r, q, :].bitcast(f32), ALU.subtract)\
                    .then_inc(dve_vlo, 1)

            def factor(r, kind, i, q):
                n = (kind * KT + i) * Q + q
                return pst[:, r, n:n + 1]

            def body(t, r, nxt, cur, prev):
                if nxt:
                    dve.wait_ge(pool_par, t + 2)
                    for i in range(KT):
                        dve.wait_ge(act_xtb, 4 * (t + 1) + i + 1)
                        for q in range(Q):
                            c = slice(q * N, (q + 1) * N)
                            last = dve.scalar_tensor_tensor(out=lo[:, i, c], in0=w_bank(i)[:, c],
                                                            scalar=factor((r + 1) % 3, SK, i, q),
                                                            in1=hi[:, i, c].bitcast(f32),
                                                            op0=ALU.mult, op1=ALU.subtract)
                        last.then_inc(dve_lo, 1)
                if cur:
                    if prev:
                        dve.wait_ge(pool_md, 4 * t)
                    for j in range(4):
                        dve.wait_ge(pe_s, 4 * t + j + 1)
                        dve.tensor_reduce(rmax[:, 16 * j:16 * (j + 1)],
                                          g_bank(j).rearrange("p (a e) -> p a e", e=32), axis=AX.X, op=ALU.max)\
                            .then_inc(dve_max, 1)
                if prev:
                    for i in range(KT):
                        dve.wait_ge(act_ahi, 4 * (t - 1) + i + 1)
                        for q in range(Q):
                            c = slice(q * N, (q + 1) * N)
                            last = dve.scalar_tensor_tensor(out=lo[:, i, c], in0=an_v[:, i, q, :],
                                                            scalar=factor((r + 2) % 3, SO, i, q),
                                                            in1=hi[:, i, c].bitcast(f32),
                                                            op0=ALU.mult, op1=ALU.subtract)
                        last.then_inc(dve_alo, 1)
                if cur:
                    for h in range(2):
                        for j in (2 * h, 2 * h + 1):
                            dve.wait_ge(act_rec, 4 * t + j + 1)
                            c = slice(512 * j, 512 * (j + 1))
                            dve.tensor_tensor(pr[:, c], pr[:, c], g_bank(j), ALU.mult).then_inc(dve_div, 1)
                        dve.wait_ge(dve_div, 4 * t + 2 * h + 2)
                        c = slice(1024 * h, 1024 * (h + 1))
                        for q in range(DQ):
                            p = slice(32 * q, 32 * (q + 1))
                            last = dve.tensor_copy(bd[p, q, c], pr[p, c])
                        last.then_inc(dve_bp, 1)
                if prev:
                    if not nxt:
                        dve.wait_ge(pe_x, 4 * (t - 1))
                    if nxt:
                        dve.wait_ge(k_moved, 256 * (t + 2))
                    for m in range(4):
                        dve.wait_ge(pe_o, 4 * (t - 1) + m + 1)
                        for q in range(Q):
                            last = dve.scalar_tensor_tensor(out=x1_v[:, m, q, :], in0=w_bank(m)[:, q * N:(q + 1) * N],
                                                            scalar=factor((r + 2) % 3, DO, m, q),
                                                            in1=xtb_v[:, (r + 2) % 3, m, q, :],
                                                            op0=ALU.mult, op1=ALU.add)
                        last.then_inc(dve_x1, 1)
                if nxt:
                    dve.wait_ge(k_moved, 256 * (t + 2))
                    if cur:
                        dve.wait_ge(pe_v, 4 * (t + 1))
                    dve.tensor_copy(kp[:, :, :, :].rearrange("p c e g -> p e c g"), kq_v).then_inc(dve_kp, 1)
                if prev:
                    dve.wait_ge(act_z, t)
                    dve.scalar_tensor_tensor(out=z_lo[:, :], in0=w_bank(0)[:, 0:N],
                                             scalar=ub_st[:, (r + 2) % 3:(r + 2) % 3 + 1],
                                             in1=z_hi[:, :].bitcast(f32), op0=ALU.add, op1=ALU.subtract)\
                        .then_inc(dve_zlo, 1)
                if nxt:
                    if cur:
                        dve.wait_ge(pe_pv, 4 * (t + 1))
                    else:
                        dve.wait_ge(zeroed, 1)
                    dve.wait_ge(dve_kp, t + 2)
                    for q in range(Q):
                        p = slice(32 * q, 32 * (q + 1))
                        last = dve.tensor_copy(bd[p, q, :], spare[p, :])
                    last.then_inc(dve_bs, 1)
                if prev:
                    for b in range(Q):
                        dve.wait_ge(pe_x, 4 * (t - 1) + b + 1)
                        dve.wait_ge(act_y, 4 * (t - 1) + b + 1)
                        dve.tensor_tensor(yb_v[:, b, :], g_bank(b), yb_v[:, b, :], ALU.add).then_inc(dve_out, 1)

            steps(dve, body)


_INS = ['x', 'cond_512', 'L0_cond_k_aff_w', 'L0_cond_k_aff_b', 'L0_cond_k_w', 'L0_cond_k_b', 'L0_cond_o_aff_w',
        'L0_cond_o_aff_b', 'L0_cond_o_w', 'L0_cond_o_b', 'L1_cond_W_dec', 'L1_cond_b_dec', 'L1_cond_V']


def kernel(**inputs):
    import numpy as _np
    import concourse.bacc as _bacc
    from concourse import mybir as _mybir
    from concourse.bass_utils import run_bass_kernel_spmd as _run

    nc = _bacc.Bacc("TRN2", target_bir_lowering=False, num_devices=1)
    arrays, args = {}, []
    for name in _INS:
        a = _np.ascontiguousarray(inputs[name])
        arrays[f"in_{name}_dram"] = a
        args.append(nc.dram_tensor(f"in_{name}_dram", a.shape, _mybir.dt.from_np(a.dtype), kind="ExternalInput").ap())
    shape = inputs['x'].shape
    args.append(nc.dram_tensor("out_0_dram", shape, _mybir.dt.float32, kind="ExternalOutput").ap())
    cond_resid_kernel(nc, *args)
    r = _run(nc, [arrays], core_ids=[0])
    return r.results[0]["out_0_dram"]
```

```python
import concourse.bass as bass
from concourse import mybir
from contextlib import ExitStack


def cond_resid_kernel(
    nc: bass.Bass,
    x: bass.AP,
    cond: bass.AP,
    k_aff_w: bass.AP,
    k_aff_b: bass.AP,
    k_w: bass.AP,
    k_b: bass.AP,
    o_aff_w: bass.AP,
    o_aff_b: bass.AP,
    o_w: bass.AP,
    o_b: bass.AP,
    W_dec: bass.AP,
    b_dec: bass.AP,
    V: bass.AP,
    out: bass.AP,
):
    f32 = mybir.dt.float32
    f32r = mybir.dt.float32r
    ALU = mybir.AluOpType
    ACT = mybir.ActivationFunctionType
    AX = mybir.AxisListType

    B, N, F = x.shape
    S = cond.shape[1]
    K = V.shape[0]
    H = 16
    D = F // H
    P = 128
    Q = 4
    T = B // Q
    KT = F // P
    ST = S // P
    TOK = Q * N
    GG = N // 8
    E = 2 * H
    GD = 1
    GA = 6
    DQ = 2
    KP = 32
    SCALE = float(D) ** -0.5
    EPS = 1e-8
    SK, DK, SO, DO = range(4)
    NPAR = 4 * KT * Q

    ctx = ExitStack()
    with ctx:
        def sb(name, shape, dt=f32):
            return ctx.enter_context(nc.sbuf_tensor(name, shape, dt))

        def sem(name):
            return ctx.enter_context(nc.semaphore(name))

        arena = sb("arena", [P, 8192 + 7 * 2048 + 2048 + 3 * 2048])
        at = [0]

        def cut(n):
            at[0] += n
            return arena[:, at[0] - n:at[0]]

        blockdiag = cut(8192)
        x1t = cut(2048)
        aq = cut(2048)
        an = cut(2048)
        pr = cut(2048)
        vt = cut(2048)
        yb = cut(2048)
        xtok = cut(2048)
        kn = cut(2048)
        xtb = cut(6144)

        bd = blockdiag.rearrange("p (c m) -> p c m", c=Q)
        bd_scores = blockdiag.rearrange("p (q e c g) -> p q e c g", q=Q, c=4, e=E)
        bd_probs = blockdiag.rearrange("p (c g q e) -> p c g q e", c=Q, g=GG, q=Q)
        kn_v = kn.rearrange("p (m q n) -> p m q n", m=KT, q=Q)
        kq_v, kq0_v = (a.rearrange("p (e c g) -> p e c g", e=E, c=4) for a in (pr, aq))
        kq_s, kq0_s = (a.rearrange("p (m k n) -> p m k n", m=KT, k=4) for a in (pr, aq))
        v_v = vt.rearrange("p (g q d) -> p g q d", g=GG, q=Q)
        aq_v = aq.rearrange("p (e c g) -> p e c g", e=E, c=4)
        aq_s = aq.rearrange("p (m k n) -> p m k n", m=KT, k=4)
        an_v = an.rearrange("p (m q n) -> p m q n", m=KT, q=Q)
        turned = x1t
        x1_v = x1t.rearrange("p (m q n) -> p m q n", m=KT, q=Q)
        yb_v = yb.rearrange("p (q f) -> p q f", q=Q)
        xtok_v = xtok.rearrange("p (q f) -> p q f", q=Q)
        xtb_v = xtb.rearrange("p (s m q n) -> p s m q n", s=3, m=KT, q=Q)

        hi = sb("hi", [P, KT, TOK], f32r)
        lo = sb("lo", [P, KT, TOK], f32r)
        w_hi = [sb(f"w_hi{n}", [P, KT, F], f32r) for n in range(2)]
        w_lo = [sb(f"w_lo{n}", [P, KT, F], f32r) for n in range(2)]
        rmax = sb("rmax", [P, GG * Q, 2])
        rsum = sb("rsum", [P, GG * Q, 2])
        rinv = sb("rinv", [P, GG * Q, 2])
        rown = sb("rown", [P, GG * Q, 2])
        par = sb("par", [P, T, NPAR])
        pst = sb("pst", [P, 3, NPAR])
        ubias = sb("ubias", [P, T])
        ub_st = sb("ub_st", [P, 3])
        ust = sb("ust", [P, KT, Q, KP])
        z = sb("z", [P, 2, N], f32r)
        v_hi = sb("v_hi", [P, 2, F], f32r)
        v_lo = sb("v_lo", [P, 2, F], f32r)
        kp = sb("kp", [P, 4, E, GG])
        ident = sb("ident", [P, P])
        own = sb("own", [P, 2])
        aff_b = sb("aff_b", [P, 2, KT])
        bias = sb("bias", [P, 2, KT])
        bdec = sb("bdec", [P, KT, K])
        wlast = sb("wlast", [P, ST, KP])
        blast = sb("blast", [P, 1])
        ct = sb("ct", [P, ST, B])

        spare = kp[:, :, :, :].rearrange("p c e g -> p (c e g)")
        dem, root, inv = (spare[:, n * 2 * KT * B:(n + 1) * 2 * KT * B].rearrange("p (w n) -> p w n", w=2)
                          for n in range(3))
        v_rep = spare[:, 3 * 2 * KT * B:3 * 2 * KT * B + F]
        sty2 = ust[:, :, :, :].rearrange("p (w f) q k -> p w (f q k)", w=2).rearrange("p w (f b) -> p w f b", b=B)
        cond_sb = kn[0:B, 0:S]
        aff_in = xtb[:, 0:2048].rearrange("p (w t s) -> p w t s", w=2, t=KT)
        aff_t = x1t.rearrange("p (w s f) -> p w s f", w=2, s=ST)
        w_in = [blockdiag[:, 2048 * n:2048 * (n + 1)].rearrange("p (t i) -> p t i", t=KT) for n in (2, 3)]
        w_sq = [a.rearrange("p (t o) -> p t o", t=KT) for a in (x1t, aq)]
        CI = 8
        CH = P // CI
        CC = CI * K
        NC = 8
        wc = [arena[:, 12288 + 4 * CC * n:12288 + 4 * CC * (n + 1)].rearrange("p (m h c) -> p m h c", m=ST, h=2)
              for n in range(NC)]
        u_raw = xtb[:, 2048:2048 + P * K]
        us = [a.rearrange("p (t q k) -> p t q k", t=T, q=Q)
              for a in (vt, yb, an, x1t)]

        u_dram = nc.dram_tensor("u_scratch", [T, P, KT, Q, KP], f32)

        Gp = ctx.enter_context(nc.psum_tensor("Gp", [P, 4, TOK], f32))
        Wp = ctx.enter_context(nc.psum_tensor("Wp", [P, 4, TOK], f32))

        def g_bank(j):
            return Gp[:, j, :]

        def w_bank(j):
            return Wp[:, j, :]

        ld_cond, ld_aff, ld_small, ld_bias, ld_v = (
            sem(n) for n in ("ld_cond", "ld_aff", "ld_small", "ld_bias", "ld_v"))
        ld_w = [sem("ld_wk"), sem("ld_wo")]
        ld_wc = [sem(f"ld_wc{n}") for n in range(NC)]
        st_u = [sem("st_u0"), sem("st_u1")]
        cleared_ident, made_ident, made_own, padded = (
            sem(n) for n in ("cleared_ident", "made_ident", "made_own", "padded"))
        zeroed = sem("zeroed")
        pe_ct, act_ct = sem("pe_ct"), sem("act_ct")
        pe_aff, act_aff = sem("pe_aff"), sem("act_aff")
        pe_sty, dve_sty, act_sty = sem("pe_sty"), sem("dve_sty"), sem("act_sty")
        pe_w, act_whi, act_wsq, dve_wlo = sem("pe_w"), sem("act_whi"), sem("act_wsq"), sem("dve_wlo")
        pe_dem, dve_dem, pool_style = sem("pe_dem"), sem("dve_dem"), sem("pool_style")
        dve_sum, act_root, dve_newton = sem("dve_sum"), sem("act_root"), sem("dve_newton")
        dve_zlo = sem("dve_zlo")
        act_vhi, dve_vlo = sem("act_vhi"), sem("dve_vlo")
        pe_ul, act_ul = sem("pe_ul"), sem("act_ul")
        pe_u, act_u, pe_ut, dve_u, dve_pad, dve_clear = (
            sem(n) for n in ("pe_u", "act_u", "pe_ut", "dve_u", "dve_pad", "dve_clear"))
        x_in = sem("x_in")
        u_in = sem("u_in")
        k0_moved = sem("k0_moved")
        k_moved, k_moved_pool = sem("k_moved"), sem("k_moved_pool")
        k_placed = sem("k_placed")
        a_moved, a_moved_pool = sem("a_moved"), sem("a_moved_pool")
        stored = [sem(f"stored{b}") for b in range(Q)]
        pe_t, pe_q, pe_s, pe_v, pe_pv, pe_o, pe_z, pe_y, pe_x = (
            sem(n) for n in ("pe_t", "pe_q", "pe_s", "pe_v", "pe_pv", "pe_o", "pe_z", "pe_y", "pe_x"))
        pe_hilo = sem("pe_hilo")
        act_hi, act_xtb, act_k, act_v, act_exp, act_aq, act_ahi, act_z, act_y, act_bp = (
            sem(n) for n in ("act_hi", "act_xtb", "act_k", "act_v", "act_exp", "act_aq", "act_ahi", "act_z", "act_y", "act_bp"))
        dve_sub, dve_rsum, dve_inv, dve_prob, dve_turned = (
            sem(n) for n in ("dve_sub", "dve_rsum", "dve_inv", "dve_prob", "dve_turned"))
        dve_lo, dve_max, dve_bp, dve_bs, dve_alo, dve_x1, dve_out, dve_kp = (
            sem(n) for n in ("dve_lo", "dve_max", "dve_bp", "dve_bs", "dve_alo", "dve_x1", "dve_out", "dve_kp"))
        pool_par, pool_ub = sem("pool_par"), sem("pool_ub")

        def steps(eng, body):
            for t in (0, 1):
                body(t, t % 3, True, True, t >= 1)
            with eng.Fori(0, (T - 4) // 3) as triple:
                for n in range(2, 5):
                    body(3 * triple + n, n % 3, True, True, True)
            for t in (T - 2, T - 1, T):
                body(t, t % 3, t < T - 1, t < T, True)

        def later(t):
            return type(t) is not int or t >= 2

        def place(n):
            return n % NC if n < CH else n % (NC // 2)

        def chunks_there(n):
            return sum(place(k) == place(n) for k in range(n + 1))

        def chunk_before(n):
            return max((k for k in range(n) if place(k) == place(n)), default=None)

        def moves_split(t):
            return type(t) is int and t in (T - 2, T - 1)

        def z_rows(b, part):
            first = KP * (2 * (b % 2) + part)
            return slice(first, first + KP)

        block = ctx.enter_context(nc.Block())

        @block.sync
        def _(sp):
            sp.dma_start(cond_sb, cond[:, :]).then_inc(ld_cond, 16)
            for w, a in enumerate((k_aff_w, o_aff_w)):
                sp.dma_start(aff_in[:, w], a.rearrange("(t p) s -> p t s", p=P)).then_inc(ld_aff, 16)
            for w, a in enumerate((k_aff_b, o_aff_b)):
                sp.dma_start(aff_b[:, w, :], a.rearrange("(t p) -> p t", p=P),
                             allow_slow_non_contiguous=True).then_inc(ld_small, 16)
            for w, a in enumerate((k_w, o_w)):
                sp.dma_start(w_in[w], a.rearrange("(t p) i -> p t i", p=P)).then_inc(ld_w[w], 16)
            for w, a in enumerate((k_b, o_b)):
                sp.dma_start(bias[:, w, :], a.rearrange("(t p) -> p t", p=P),
                             allow_slow_non_contiguous=True).then_inc(ld_bias, 16)
            for n in range(2 * CH):
                pair, ch = n // CH, n % CH
                if chunk_before(n) is not None:
                    sp.wait_ge(pe_u, chunk_before(n) + 1)
                src = W_dec[:, 2 * pair * P * K:2 * (pair + 1) * P * K].rearrange("(m p) (h c) -> p m h c", p=P, h=2)
                for m in range(ST):
                    sp.dma_start(wc[place(n)][:, m], src[:, m, :, ch * CC:(ch + 1) * CC]).then_inc(ld_wc[place(n)], 16)
                if n == 3:
                    sp.dma_start(xtok_v, x[0:Q].rearrange("q n f -> n q f")).then_inc(x_in, 16)
                if n == 13:
                    sp.wait_ge(pe_t, 4)
                    sp.dma_start(xtok_v, x[Q:2 * Q].rearrange("q n f -> n q f")).then_inc(x_in, 16)
            for it in range(KT):
                sp.wait_ge(dve_u, 16 * (it // 2 + 1))
                sp.dma_start(u_dram[:, :, it, :, :].rearrange("t p q k -> p t q k"), us[it]).then_inc(st_u[it // 2], 16)
            for pair in range(2):
                sp.wait_ge(st_u[pair], 32)

            def body(t, r, nxt, cur, prev):
                static = type(t) is int
                at_once = (lambda v: v) if static else sp.to_reg
                t_of_next, k_of_next = at_once(4 * (t + 2)), at_once(4 * (t + 2))
                aq_made, tiles_before = at_once(4 * (t + 1)), at_once(4 * t)
                turned_halves, steps_before = at_once(2 * (t + 1)), at_once(t)
                k_came, k_came_pool = at_once(64 * (4 - GD) * (t + 1)), at_once(64 * GD * (t + 1))
                sums_formed = at_once(4 * (t + 1))
                outs = [at_once(4 * (t - 1) + b + 1) for b in range(Q)]
                if nxt:
                    if not static or t < T - 2:
                        sp.wait_ge(pe_t, t_of_next)
                        sp.dma_start(xtok_v, x[bass.ds(Q * (t + 2), Q)].rearrange("q n f -> n q f")).then_inc(x_in, 16)
                    sp.wait_ge(act_k, k_of_next)
                    sp.wait_ge(dve_turned, turned_halves)
                    for k in range(4 - GD):
                        for q in range(Q):
                            sp.dma_start(kq_s[D * q:D * (q + 1), :, k, :], kn_v[D * k:D * (k + 1), :, q, :])\
                              .then_inc(k_moved, 16)
                    sp.wait_ge(k_moved, k_came)
                    sp.wait_ge(k_moved_pool, k_came_pool)
                    sp.wait_ge(pe_pv, sums_formed)
                    for q in range(Q):
                        p = slice(32 * q, 32 * (q + 1))
                        sp.dma_start(bd[p, q, :], pr[p, :]).then_inc(k_placed, 16)
                if cur:
                    sp.wait_ge(act_aq, aq_made)
                    if prev:
                        sp.wait_ge(act_ahi, tiles_before)
                        sp.wait_ge(dve_alo, tiles_before)
                    for n in range(16 - GA if moves_split(t) else 16):
                        k, q = n // Q, n % Q
                        sp.dma_start(an_v[D * k:D * (k + 1), :, q, :], aq_s[D * q:D * (q + 1), :, k, :])\
                          .then_inc(a_moved, 16)
                    if prev:
                        sp.wait_ge(pe_z, steps_before)
                    sp.dma_start(ust[:, :, :, :], u_dram[t]).then_inc(u_in, 16)
                if prev:
                    for b in range(Q):
                        sp.wait_ge(dve_out, outs[b])
                        sp.dma_start(out[Q * (t - 1) + b], yb_v[:, b, :]).then_inc(stored[b], 16)

            steps(sp, body)
            for b in range(Q):
                sp.wait_ge(stored[b], 16 * T)

        @block.gpsimd
        def _(pool):
            pool.memset(ident[:, :], 0.0).then_inc(cleared_ident, 1)
            pool.wait_ge(cleared_ident, 1)
            pool.affine_select(out=ident[:, :], in_=ident[:, :], compare_op=ALU.not_equal, fill=1.0, base=0,
                               pattern=[[-1, P]], channel_multiplier=1).then_inc(made_ident, 1)
            pool.memset(wlast[:, :, :], 0.0).then_inc(padded, 1)
            pool.memset(blast[:, :], 0.0).then_inc(padded, 1)
            pool.memset(v_rep, 0.0).then_inc(padded, 1)
            pool.wait_ge(padded, 3)
            pool.dma_start(wlast[:, :, 0:K], W_dec[:, F * K:(F + 1) * K].rearrange("(m p) k -> p m k", p=P))\
                .then_inc(ld_v, 16)
            pool.dma_start(bdec[:, :, :], b_dec[0:F * K].rearrange("(t p k) -> p t k", p=P, k=K)).then_inc(ld_v, 16)
            for q in range(Q):
                pool.dma_start(blast[KP * q:KP * q + K, :], b_dec[F * K:(F + 1) * K].rearrange("(k a) -> k a", a=1))\
                    .then_inc(ld_v, 16)
                pool.dma_start(v_rep[KP * q:KP * q + K, :], V[:, :]).then_inc(ld_v, 16)
            pool.wait_ge(dve_sty, 2)
            pool.tensor_copy(pst[:, 0, 0:KT * Q], par[:, 0, 0:KT * Q]).then_inc(pool_style, 1)
            pool.memset(blockdiag[:, 0:4096], 0.0).then_inc(zeroed, 1)
            pool.wait_ge(pe_w, 8)
            pool.memset(blockdiag[:, 4096:8192], 0.0).then_inc(zeroed, 1)
            pool.wait_ge(dve_dem, 1)
            pool.tensor_copy(pst[:, 0, KT * Q:2 * KT * Q], par[:, 0, KT * Q:2 * KT * Q]).then_inc(pool_style, 1)
            pool.wait_ge(dve_dem, 2)
            pool.tensor_copy(pst[:, 0, 2 * KT * Q:NPAR], par[:, 0, 2 * KT * Q:NPAR]).then_inc(pool_par, 1)
            pool.wait_ge(act_k, 4)
            for k in range(4):
                for q in range(Q):
                    pool.dma_start(kq0_s[D * q:D * (q + 1), :, k, :], kn_v[D * k:D * (k + 1), :, q, :])\
                        .then_inc(k0_moved, 16)
            pool.wait_ge(act_ul, 1)

            def body(t, r, nxt, cur, prev):
                if nxt:
                    if later(t):
                        pool.wait_ge(dve_x1, 4 * (t - 1))
                    pool.tensor_copy(pst[:, (r + 1) % 3, :],
                                     par[:, bass.ds(t + 1, 1), :].rearrange("p a n -> p (a n)")).then_inc(pool_par, 1)
                if cur:
                    if later(t):
                        pool.wait_ge(dve_zlo, 4 * (t - 1))
                    if nxt:
                        pool.wait_ge(act_k, 4 * (t + 2))
                        pool.wait_ge(dve_turned, 2 * (t + 1))
                    pool.tensor_copy(ub_st[:, r:r + 1], ubias[:, bass.ds(t, 1)]).then_inc(pool_ub, 1)
                if nxt:
                    for k in range(4 - GD, 4):
                        for q in range(Q):
                            pool.dma_start(kq_s[D * q:D * (q + 1), :, k, :], kn_v[D * k:D * (k + 1), :, q, :])\
                                .then_inc(k_moved_pool, 16)
                if moves_split(t):
                    pool.wait_ge(act_aq, 4 * (t + 1))
                    pool.wait_ge(act_ahi, 4 * t)
                    pool.wait_ge(dve_alo, 4 * t)
                    for n in range(16 - GA, 16):
                        k, q = n // Q, n % Q
                        pool.dma_start(an_v[D * k:D * (k + 1), :, q, :], aq_s[D * q:D * (q + 1), :, k, :])\
                            .then_inc(a_moved_pool, 16)

            steps(pool, body)

        @block.tensor
        def _(pe):
            pe.wait_ge(made_ident, 1)
            pe.wait_ge(ld_cond, 16)
            for s in range(ST):
                last = pe.transpose(w_bank(0)[:, s * B:(s + 1) * B], cond_sb[:, s * P:(s + 1) * P], ident[0:B, 0:B])
            last.then_inc(pe_ct, 1)
            pe.wait_ge(ld_aff, 32)
            for w in range(2):
                for s in range(ST):
                    for f in range(KT):
                        last = pe.transpose(g_bank(2 * w + s)[:, f * P:(f + 1) * P],
                                            aff_in[:, w, f, s * P:(s + 1) * P], ident[:, :])
                    last.then_inc(pe_aff, 1)
            pe.wait_ge(act_ct, 1)
            for w in range(2):
                pe.wait_ge(act_aff, 2 * w + 2)
                for f in range(KT):
                    for s in range(ST):
                        last = pe.matmul(w_bank(w)[:, f * B:(f + 1) * B], aff_t[:, w, s, f * P:(f + 1) * P],
                                         ct[:, s, :], start=(s == 0), stop=(s == ST - 1))
                last.then_inc(pe_sty, 1)

            def u_chunk(n):
                pe.wait_ge(ld_wc[place(n)], 32 * chunks_there(n))
                if n >= 2:
                    pe.wait_ge(act_u, n - 1)
                for m in range(ST):
                    for h in range(2):
                        last = pe.matmul(w_bank(2 + n % 2)[B * h:B * (h + 1), 0:CC], ct[:, m, :], wc[place(n)][:, m, h, :],
                                         start=(m == 0), stop=(m == ST - 1))
                last.then_inc(pe_u, 1)

            def transpose_u(pair):
                pe.wait_ge(act_u, CH * (pair + 1))
                for n in range(8):
                    if pair or n >= 4:
                        pe.wait_ge(dve_u, 2 * (8 * pair + n - 3))
                    else:
                        pe.wait_ge(act_k, n + 1)
                    for k in range(4 * n, min(4 * n + 4, K)):
                        last = pe.transpose(g_bank(n % 4)[:, (k % 4) * P:(k % 4 + 1) * P],
                                            u_raw.rearrange("p (i k) -> p i k", k=K)[:, :, k], ident[:, :])
                    last.then_inc(pe_ut, 1)

            def demodulation(w, o):
                if o == 0:
                    pe.wait_ge(act_wsq, 4 * (w + 1))
                    pe.wait_ge(dve_sty, 2)
                for i in range(KT):
                    last = pe.matmul(w_bank(w)[:, o * B:(o + 1) * B], w_sq[w][:, i, o * P:(o + 1) * P],
                                     sty2[:, w, i, :], start=(i == 0), stop=(i == KT - 1))
                if o == KT - 1:
                    last.then_inc(pe_dem, 1)

            def project(w, tiles, bank, done, bank_free, part_ready, part_used=None):
                for i in range(KT):
                    part_ready(i)
                    for m in tiles:
                        if i == 0:
                            bank_free(m)
                        for n, (a, b) in enumerate(((w_hi, hi), (w_hi, lo), (w_lo, hi))):
                            last = pe.matmul(bank(m), a[w][:, i, m * P:(m + 1) * P], b[:, i, :],
                                             start=(i == 0 and n == 0), stop=(i == KT - 1 and n == 2))
                        if i == KT - 1:
                            last.then_inc(done, 1)
                    if part_used is not None and i < KT - 1:
                        last.then_inc(part_used, 1)

            for w in range(2):
                pe.wait_ge(ld_w[w], 16)
                for i in range(KT):
                    if w == 1:
                        pe.wait_ge(dve_wlo, i + 1)
                        if i == 2:
                            u_chunk(1)
                    for o in range(KT):
                        last = pe.transpose(g_bank(i)[:, o * P:(o + 1) * P], w_in[w][:, o, i * P:(i + 1) * P],
                                            ident[:, :])
                    last.then_inc(pe_w, 1)
                if w == 0:
                    u_chunk(0)
            u_chunk(2)
            u_chunk(3)
            for o in range(KT):
                demodulation(0, o)
                u_chunk(4 + o)
            pe.wait_ge(x_in, 16)
            for i in range(KT):
                pe.wait_ge(dve_wlo, 4 + i + 1)
                for q in range(Q):
                    last = pe.transpose(g_bank(i)[:, q * N:(q + 1) * N], xtok_v[:, q, i * P:(i + 1) * P], ident[:, :])
                last.then_inc(pe_t, 1)
            for o in range(KT):
                demodulation(1, o)
                u_chunk(8 + o)
            for m in range(KT):
                def bank_free(m):
                    pe.wait_ge(dve_lo, m + 1)

                def part_ready(i):
                    if m == 0:
                        pe.wait_ge(act_hi, i + 1)
                        pe.wait_ge(dve_lo, i + 1)

                project(0, (m,), g_bank, pe_q, bank_free, part_ready, pe_hilo if m == 3 else None)
            for n in range(12, CH):
                u_chunk(n)
            pe.wait_ge(ld_v, 16 * (2 + 2 * Q))
            pe.wait_ge(dve_sum, 2)
            for q in range(Q):
                for s in range(ST):
                    last = pe.matmul(w_bank(0)[KP * q:KP * (q + 1), 0:T], wlast[:, s, :],
                                     ct[:, s, :].rearrange("p (t q) -> p t q", q=Q)[:, :, q],
                                     start=(s == 0), stop=(s == ST - 1))
            last.then_inc(pe_ul, 1)
            transpose_u(0)
            for n in range(CH, 2 * CH):
                u_chunk(n)
            transpose_u(1)

            def body(t, r, nxt, cur, prev):
                def second_layer_left(bank):
                    pe.wait_ge(act_y, 4 * (t - 2) + bank + 1)

                if nxt:
                    pe.wait_ge(x_in, 16 * (t + 2))
                    for i in range(KT):
                        if later(t):
                            second_layer_left(i)
                        elif t == 1:
                            pe.wait_ge(act_k, 4 + i + 1)
                        else:
                            pe.wait_ge(act_u, 2 * CH)
                            pe.wait_ge(act_ul, 1)
                        for q in range(Q):
                            last = pe.transpose(w_bank(i)[:, q * N:(q + 1) * N], xtok_v[:, q, i * P:(i + 1) * P],
                                                ident[:, :])
                        last.then_inc(pe_t, 1)
                if cur:
                    pe.wait_ge(dve_kp, t + 1)
                    if prev:
                        pe.wait_ge(k_placed, 64 * t)
                    else:
                        pe.wait_ge(dve_bs, 1)
                    for j in range(4):
                        if later(t):
                            pe.wait_ge(dve_out, 4 * (t - 2) + j + 1)
                        elif prev:
                            pe.wait_ge(act_aq, 4 * (t - 1) + j + 1)
                        else:
                            pe.wait_ge(dve_u, 32)
                        for g in range(4 * j, 4 * j + 4):
                            for c in range(4):
                                last = pe.matmul(g_bank(j)[32 * c:32 * (c + 1), (g % 4) * P:(g % 4 + 1) * P],
                                                 kp[:, c, :, g], bd_scores[:, :, :, c, g],
                                                 start=True, stop=True)
                        last.then_inc(pe_s, 1)
                    for j in range(4):
                        if nxt:
                            pe.wait_ge(act_xtb, 4 * (t + 1) + j + 1)
                            pe.wait_ge(dve_lo, 4 * (t + 1) + j + 1)
                        else:
                            second_layer_left(j)
                        for g in range(4 * j, 4 * j + 4):
                            last = pe.transpose(w_bank(j)[:, (g % 4) * P:(g % 4 + 1) * P],
                                                kp[:, :, :, g].rearrange("p c e -> p (c e)"), ident[:, :])
                        last.then_inc(pe_v, 1)

                def k_projection(*tiles):
                    def bank_free(m):
                        pe.wait_ge(act_v, 4 * t + m + 1)

                    def part_ready(i):
                        if 0 in tiles:
                            pe.wait_ge(act_hi, 4 * (t + 1) + i + 1)
                            pe.wait_ge(dve_lo, 4 * (t + 1) + i + 1)

                    project(0, tiles, w_bank, pe_q, bank_free, part_ready, pe_hilo if 3 in tiles else None)

                if nxt:
                    k_projection(0)
                    k_projection(1)
                if nxt:
                    k_projection(2, 3)
                if prev:
                    def bank_free(m):
                        if nxt:
                            pe.wait_ge(act_k, 4 * (t + 1) + m + 1)
                        elif cur:
                            pe.wait_ge(act_v, 4 * t + m + 1)
                        else:
                            second_layer_left(m)

                    def part_ready(i):
                        pe.wait_ge(act_ahi, 4 * (t - 1) + i + 1)
                        pe.wait_ge(dve_alo, 4 * (t - 1) + i + 1)

                    for tiles in ((0, 1), (2,), (3,)):
                        project(1, tiles, w_bank, pe_o, bank_free, part_ready)
                if cur:
                    pe.wait_ge(act_v, 4 * (t + 1))
                    for j in range(4):
                        if j % 2 == 0:
                            pe.wait_ge(dve_bp, 2 * t + j // 2 + 1)
                            pe.wait_ge(act_bp, 2 * t + j // 2 + 1)
                        for g in range(4 * j, 4 * j + 4):
                            for q in range(Q):
                                last = pe.matmul(g_bank(j)[32 * q:32 * (q + 1), (g % 4) * P:(g % 4 + 1) * P],
                                                 v_v[:, g, q, :], bd_probs[:, :, g, q, :], start=True, stop=True)
                        last.then_inc(pe_pv, 1)
                if prev:
                    pe.wait_ge(dve_x1, 4 * t)
                    pe.wait_ge(u_in, 16 * t)
                    for i in range(KT):
                        for q in range(Q):
                            last = pe.matmul(w_bank(0)[KP * q:KP * (q + 1), 0:N], ust[:, i, q, :],
                                             x1_v[:, i, q, :], start=(i == 0), stop=(i == KT - 1))
                    last.then_inc(pe_z, 1)
                    for b in range(Q):
                        if cur:
                            pe.wait_ge(act_aq, 4 * t + b + 1)
                        else:
                            pe.wait_ge(dve_out, 4 * (t - 2) + b + 1)
                        for i in range(KT):
                            last = pe.transpose(g_bank(b)[:, i * P:(i + 1) * P], x1_v[:, i, b, :], ident[:, :])
                        last.then_inc(pe_x, 1)
                    pe.wait_ge(dve_zlo, 4 * t)
                    for b in range(Q):
                        for n, v in enumerate((v_hi, v_lo)):
                            last = pe.matmul(w_bank(b), z[:, b // 2, :], v[:, b % 2, :], start=(n == 0), stop=(n == 1))
                        last.then_inc(pe_y, 1)

            steps(pe, body)

        @block.scalar
        def _(act):
            act.wait_ge(pe_ct, 1)
            act.activation(ct[:, :, :].rearrange("p s b -> p (s b)"), w_bank(0)[:, 0:ST * B], ACT.Copy)\
                .then_inc(act_ct, 1)
            for n in range(4):
                act.wait_ge(pe_aff, n + 1)
                act.activation(aff_t[:, n // 2, n % 2, :], g_bank(n), ACT.Copy).then_inc(act_aff, 1)
            act.wait_ge(ld_small, 32)
            for w in range(2):
                act.wait_ge(pe_sty, w + 1)
                for f in range(KT):
                    last = act.activation(sty2[:, w, f, :], w_bank(w)[:, f * B:(f + 1) * B], ACT.Square,
                                          bias=aff_b[:, w, f:f + 1])
                last.then_inc(act_sty, 1)

            def raw_u(n):
                ch = n % CH
                act.wait_ge(pe_u, n + 1)
                if n == CH:
                    act.wait_ge(pe_ut, 8)
                act.activation(u_raw[:, ch * CC:(ch + 1) * CC], w_bank(2 + n % 2)[:, 0:CC], ACT.Copy)\
                    .then_inc(act_u, 1)

            for w in range(2):
                for i in range(KT):
                    act.wait_ge(pe_w, 4 * w + i + 1)
                    act.activation(w_hi[w][:, i, :], g_bank(i), ACT.Copy).then_inc(act_whi, 1)
                    act.activation(w_sq[w][:, i, :], g_bank(i), ACT.Square).then_inc(act_wsq, 1)
                    if (w, i) == (0, 3):
                        raw_u(0)
                    if (w, i) == (1, 1):
                        raw_u(1)
            for n in range(2, 8):
                raw_u(n)
            act.wait_ge(pool_style, 1)
            act.wait_ge(ld_bias, 32)
            for i in range(KT):
                act.wait_ge(pe_t, i + 1)
                for q in range(Q):
                    n = i * Q + q
                    last = act.activation(hi[:, i, q * N:(q + 1) * N], g_bank(i)[:, q * N:(q + 1) * N],
                                          ACT.Copy, scale=pst[:, 0, n:n + 1])
                last.then_inc(act_hi, 1)
                act.activation(xtb_v[:, 0, i].rearrange("p q n -> p (q n)"), g_bank(i), ACT.Identity,
                               bias=bias[:, 1, i:i + 1]).then_inc(act_xtb, 1)
                if i > 0:
                    raw_u(7 + i)
            for w in range(2):
                if w:
                    raw_u(11)
                act.wait_ge(dve_sum, w + 1)
                act.activation(root[:, w, :], dem[:, w, :], ACT.Sqrt).then_inc(act_root, 1)
            act.preload_act_table_set("natural_log_exp_and_others")
            act.wait_ge(pool_style, 2)
            for m in range(KT):
                act.wait_ge(pe_q, m + 1)
                for q in range(Q):
                    n = (DK * KT + m) * Q + q
                    last = act.activation(kn_v[:, m, q, :], g_bank(m)[:, q * N:(q + 1) * N], ACT.Identity,
                                          bias=bias[:, 0, m:m + 1], scale=pst[:, 0, n:n + 1])
                last.then_inc(act_k, 1)
            for n in range(12, CH):
                raw_u(n)
            act.wait_ge(ld_v, 16 * (2 + 2 * Q))
            act.wait_ge(pe_ul, 1)
            act.activation(ubias[:, :], w_bank(0)[:, 0:T], ACT.Identity, bias=blast[:, :]).then_inc(act_ul, 1)
            act.wait_ge(dve_clear, 1)
            for s in range(2):
                r = slice(2 * KP * s, 2 * KP * (s + 1))
                act.activation(v_hi[r, s, :], v_rep[r, :], ACT.Copy).then_inc(act_vhi, 1)
            for n in range(CH, 2 * CH):
                raw_u(n)

            def factor(r, kind, i, q):
                n = (kind * KT + i) * Q + q
                return pst[:, r, n:n + 1]

            def body(t, r, nxt, cur, prev):
                def result_moved():
                    by_pool = 0 if type(t) is not int else max(0, t - (T - 2))
                    act.wait_ge(a_moved, 256 * t - 16 * GA * by_pool)
                    if by_pool:
                        act.wait_ge(a_moved_pool, 16 * GA * by_pool)

                def x_with_bias(i):
                    act.wait_ge(dve_lo, 4 * (t + 1) + i + 1)
                    act.activation(xtb_v[:, (r + 1) % 3, i].rearrange("p q n -> p (q n)"), w_bank(i), ACT.Identity,
                                   bias=bias[:, 1, i:i + 1]).then_inc(act_xtb, 1)

                if nxt:
                    act.wait_ge(pool_par, t + 2)
                    if later(t):
                        act.wait_ge(pe_o, 4 * (t - 1))
                        act.wait_ge(dve_x1, 4 * (t - 1))
                    else:
                        act.wait_ge(pe_q, 4 * (t + 1))
                    for i in range(KT):
                        act.wait_ge(pe_t, 4 * (t + 1) + i + 1)
                        for q in range(Q):
                            last = act.activation(hi[:, i, q * N:(q + 1) * N], w_bank(i)[:, q * N:(q + 1) * N],
                                                  ACT.Copy, scale=factor((r + 1) % 3, SK, i, q))
                        last.then_inc(act_hi, 1)
                        if i == 2:
                            x_with_bias(0)
                    for i in range(1, KT):
                        x_with_bias(i)
                if cur:
                    if prev:
                        act.wait_ge(pe_pv, 4 * t)
                    else:
                        act.wait_ge(st_u[0], 32)
                    for j in range(4):
                        act.wait_ge(pe_v, 4 * t + j + 1)
                        act.activation(vt[:, 512 * j:512 * (j + 1)], w_bank(j), ACT.Copy).then_inc(act_v, 1)

                def k_out(m):
                    act.wait_ge(pe_q, 4 * (t + 1) + m + 1)
                    for q in range(Q):
                        last = act.activation(kn_v[:, m, q, :], w_bank(m)[:, q * N:(q + 1) * N], ACT.Identity,
                                              bias=bias[:, 0, m:m + 1], scale=factor((r + 1) % 3, DK, m, q))
                    last.then_inc(act_k, 1)

                if cur:
                    for h in range(2):
                        act.wait_ge(dve_sub, 4 * t + 2 * h + 2)
                        c = slice(1024 * h, 1024 * (h + 1))
                        act.activation(pr[:, c], pr[:, c], ACT.Exp, scale=SCALE).then_inc(act_exp, 1)

                def attended_hi(i):
                    if i == 0:
                        result_moved()
                    if not nxt:
                        act.wait_ge(pe_o, 4 * (t - 1))
                    elif i < KT - 1:
                        act.wait_ge(pe_hilo, 3 * (t + 1) + i + 1)
                    else:
                        act.wait_ge(pe_q, 4 * (t + 2))
                    for q in range(Q):
                        last = act.activation(hi[:, i, q * N:(q + 1) * N], an_v[:, i, q, :], ACT.Copy,
                                              scale=factor((r + 2) % 3, SO, i, q))
                    last.then_inc(act_ahi, 1)

                if nxt:
                    if prev:
                        act.wait_ge(k_moved, 64 * (4 - GD) * t)
                        act.wait_ge(k_moved_pool, 64 * GD * t)
                    else:
                        act.wait_ge(k0_moved, 256)
                    k_out(0)
                    k_out(1)
                if prev:
                    for i in range(KT):
                        attended_hi(i)
                if nxt:
                    k_out(2)
                    k_out(3)
                if cur:
                    for h in range(2):
                        act.wait_ge(dve_turned, 2 * t + h + 1)
                        c = slice(1024 * h, 1024 * (h + 1))
                        for q in range(DQ if prev else Q - 1, Q):
                            p = slice(32 * q, 32 * (q + 1))
                            last = act.activation(bd[p, q, c], turned[p, c], ACT.Copy)
                        last.then_inc(act_bp, 1)
                    if not prev:
                        act.wait_ge(dve_kp, 1)
                        act.wait_ge(dve_bs, 1)
                    else:
                        result_moved()
                    for j in range(4):
                        act.wait_ge(pe_pv, 4 * t + j + 1)
                        act.activation(aq_v[:, :, :, 4 * j:4 * (j + 1)],
                                       g_bank(j).rearrange("p (g c e) -> p e c g", g=4, c=4), ACT.Copy)\
                            .then_inc(act_aq, 1)
                if prev:
                    act.wait_ge(pe_z, t)
                    act.wait_ge(pool_ub, t)
                    if later(t):
                        act.wait_ge(pe_y, 4 * (t - 1))
                    for b in range(Q):
                        p = slice(KP * b, KP * (b + 1))
                        act.activation(z[z_rows(b, 0), b // 2, :], w_bank(0)[p, 0:N], ACT.Identity,
                                       bias=ub_st[p, (r + 2) % 3:(r + 2) % 3 + 1]).then_inc(act_z, 1)
                if prev:
                    for b in range(Q):
                        act.wait_ge(pe_y, 4 * (t - 1) + b + 1)
                        if later(t):
                            act.wait_ge(stored[b], 16 * (t - 1))
                        act.activation(yb_v[:, b, :], w_bank(b), ACT.Copy).then_inc(act_y, 1)

            steps(act, body)

        @block.vector
        def _(dve):
            dve.memset(v_hi[:, :, :].bitcast(f32), 0.0).then_inc(dve_clear, 1)
            dve.memset(v_lo[:, :, :].bitcast(f32), 0.0).then_inc(dve_pad, 1)
            dve.wait_ge(made_ident, 1)
            dve.tensor_reduce(own[:, :], ident[:, :].rearrange("p (a n) -> p n a", n=2), axis=AX.X, op=ALU.add)\
                .then_inc(made_own, 1)
            dve.wait_ge(made_own, 1)
            pv = par[:, :, :].rearrange("p t (k f q) -> p k f t q", k=4, f=KT)
            dve.wait_ge(ld_small, 32)
            for w in range(2):
                dve.wait_ge(act_sty, w + 1)
                for f in range(KT):
                    last = dve.tensor_scalar(pv[:, (SK, SO)[w], f],
                                             w_bank(w)[:, f * B:(f + 1) * B].rearrange("p (t q) -> p t q", q=Q),
                                             aff_b[:, w, f:f + 1], None, ALU.add)
                last.then_inc(dve_sty, 1)
            for w in range(2):
                for i in range(KT):
                    dve.wait_ge(act_wsq, 4 * w + i + 1)
                    dve.tensor_tensor(w_lo[w][:, i, :], g_bank(i), w_hi[w][:, i, :].bitcast(f32), ALU.subtract)\
                        .then_inc(dve_wlo, 1)

            def add_eps(w):
                dve.wait_ge(pe_dem, w + 1)
                dve.tensor_scalar(dem[:, w, :], w_bank(w)[:, 0:KT * B], EPS, None, ALU.add).then_inc(dve_sum, 1)

            def demodulate(w):
                dve.wait_ge(act_root, w + 1)
                dve.reciprocal(inv[:, w, :], root[:, w, :]).then_inc(dve_newton, 1)
                dve.wait_ge(dve_newton, 4 * w + 1)
                dve.tensor_tensor(root[:, w, :], inv[:, w, :], inv[:, w, :], ALU.mult).then_inc(dve_newton, 1)
                dve.wait_ge(dve_newton, 4 * w + 2)
                dve.tensor_tensor(root[:, w, :], root[:, w, :], dem[:, w, :], ALU.mult).then_inc(dve_newton, 1)
                dve.wait_ge(dve_newton, 4 * w + 3)
                dve.tensor_scalar(root[:, w, :], root[:, w, :], -0.5, 1.5, ALU.mult, ALU.add).then_inc(dve_newton, 1)
                dve.wait_ge(dve_newton, 4 * w + 4)
                for f in range(KT):
                    c = slice(f * B, (f + 1) * B)
                    last = dve.tensor_tensor(pv[:, (DK, DO)[w], f],
                                             inv[:, w, c].rearrange("p (t q) -> p t q", q=Q),
                                             root[:, w, c].rearrange("p (t q) -> p t q", q=Q), ALU.mult)
                last.then_inc(dve_dem, 1)

            def u_with_bias(pair):
                for n in range(8):
                    ks = min(4, K - 4 * n)
                    dve.wait_ge(pe_ut, 8 * pair + n + 1)
                    for h in range(2):
                        dve.tensor_tensor(us[2 * pair + h][:, :, :, 4 * n:4 * n + ks].rearrange("p t q k -> p (t q) k"),
                                          g_bank(n % 4)[:, 0:ks * P].rearrange("p (k h b) -> p h b k", h=2, b=B)[:, h],
                                          bdec[:, 2 * pair + h, 4 * n:4 * n + ks].unsqueeze(1).to_broadcast([P, B, ks]),
                                          ALU.add).then_inc(dve_u, 1)

            add_eps(0)
            for i in range(KT):
                dve.wait_ge(act_xtb, i + 1)
                for q in range(Q):
                    c = slice(q * N, (q + 1) * N)
                    n = i * Q + q
                    last = dve.scalar_tensor_tensor(out=lo[:, i, c], in0=g_bank(i)[:, c], scalar=pst[:, 0, n:n + 1],
                                                    in1=hi[:, i, c].bitcast(f32), op0=ALU.mult, op1=ALU.subtract)
                last.then_inc(dve_lo, 1)
            demodulate(0)
            add_eps(1)
            demodulate(1)
            dve.wait_ge(pe_u, CH)
            for n in range(2):
                dve.memset(us[n][:, :, :, K:KP], 0.0).then_inc(dve_pad, 1)
            dve.wait_ge(dve_pad, 3)
            dve.wait_ge(ld_v, 16 * (2 + 2 * Q))
            u_with_bias(0)
            for s in range(2):
                r = z_rows(s, 0)
                dve.wait_ge(act_vhi, s + 1)
                dve.tensor_tensor(v_lo[r, s, :], v_rep[r, :], v_hi[r, s, :].bitcast(f32), ALU.subtract)\
                    .then_inc(dve_vlo, 1)
            dve.wait_ge(k0_moved, 256)
            dve.wait_ge(dve_vlo, 2)
            dve.tensor_copy(kp[:, :, :, :].rearrange("p c e g -> p e c g"), kq0_v).then_inc(dve_kp, 1)
            dve.wait_ge(zeroed, 2)
            dve.wait_ge(dve_kp, 1)
            for q in range(Q):
                p = slice(32 * q, 32 * (q + 1))
                last = dve.tensor_copy(bd[p, q, :], aq[p, :])
            last.then_inc(dve_bs, 1)
            dve.wait_ge(pe_u, 2 * CH)
            for n in range(2, 4):
                dve.memset(us[n][:, :, :, K:KP], 0.0).then_inc(dve_pad, 1)
            dve.wait_ge(dve_pad, 5)
            u_with_bias(1)

            def factor(r, kind, i, q):
                n = (kind * KT + i) * Q + q
                return pst[:, r, n:n + 1]

            def by_token(a):
                return a.rearrange("p (a h n) -> p a h n", h=H, n=2)

            def along_heads(a):
                return a.unsqueeze(2).to_broadcast([P, a.shape[1], H, 2])

            def body(t, r, nxt, cur, prev):
                def styled_lo(i):
                    dve.wait_ge(act_hi, 4 * (t + 1) + i + 1)
                    for q in range(Q):
                        c = slice(q * N, (q + 1) * N)
                        last = dve.scalar_tensor_tensor(out=lo[:, i, c], in0=w_bank(i)[:, c],
                                                        scalar=factor((r + 1) % 3, SK, i, q),
                                                        in1=hi[:, i, c].bitcast(f32),
                                                        op0=ALU.mult, op1=ALU.subtract)
                    last.then_inc(dve_lo, 1)

                def row_maxima(j):
                    dve.wait_ge(pe_s, 4 * t + j + 1)
                    dve.tensor_reduce(rmax[:, 16 * j:16 * (j + 1)],
                                      g_bank(j).rearrange("p (a h n) -> p a n h", h=H, n=2), axis=AX.X, op=ALU.max)\
                        .then_inc(dve_max, 1)

                def attended_lo(i):
                    dve.wait_ge(act_ahi, 4 * (t - 1) + i + 1)
                    for q in range(Q):
                        c = slice(q * N, (q + 1) * N)
                        last = dve.scalar_tensor_tensor(out=lo[:, i, c], in0=an_v[:, i, q, :],
                                                        scalar=factor((r + 2) % 3, SO, i, q),
                                                        in1=hi[:, i, c].bitcast(f32),
                                                        op0=ALU.mult, op1=ALU.subtract)
                    last.then_inc(dve_alo, 1)

                if nxt:
                    dve.wait_ge(pool_par, t + 2)
                    styled_lo(0)
                    styled_lo(1)
                    styled_lo(2)
                if cur:
                    row_maxima(0)
                if nxt:
                    styled_lo(3)
                if cur:
                    row_maxima(1)
                    row_maxima(2)
                    row_maxima(3)
                    if prev:
                        dve.wait_ge(dve_kp, t + 1)
                    for j in range(4):
                        dve.wait_ge(dve_max, 4 * t + j + 1)
                        c = slice(512 * j, 512 * (j + 1))
                        dve.tensor_tensor(by_token(pr[:, c]), by_token(g_bank(j)), along_heads(rmax[:, 16 * j:16 * (j + 1)]),
                                          ALU.subtract).then_inc(dve_sub, 1)
                    for h in range(2):
                        dve.wait_ge(act_exp, 2 * t + h + 1)
                        dve.tensor_reduce(rsum[:, 32 * h:32 * (h + 1)],
                                          pr[:, 1024 * h:1024 * (h + 1)].rearrange("p (a h n) -> p a n h", h=H, n=2),
                                          axis=AX.X, op=ALU.add).then_inc(dve_rsum, 1)
                    if not nxt:
                        attended_lo(0)
                        attended_lo(1)
                    dve.wait_ge(dve_rsum, 2 * t + 2)
                    dve.reciprocal(rinv[:, :, :], rsum[:, :, :]).then_inc(dve_inv, 1)
                    dve.wait_ge(dve_inv, 2 * t + 1)
                    dve.tensor_tensor(rown[:, :, :], rinv[:, :, :],
                                      own[:, :].unsqueeze(1).to_broadcast([P, GG * Q, 2]), ALU.mult).then_inc(dve_inv, 1)
                    if not nxt:
                        attended_lo(2)
                        attended_lo(3)
                    dve.wait_ge(dve_inv, 2 * t + 2)
                    for h in range(2):
                        c = slice(1024 * h, 1024 * (h + 1))
                        dve.tensor_tensor(by_token(pr[:, c]), by_token(pr[:, c]), along_heads(rown[:, 32 * h:32 * (h + 1)]),
                                          ALU.mult).then_inc(dve_prob, 1)
                        if prev and nxt and h == 0:
                            attended_lo(0)

                def turn(h):
                    dve.wait_ge(dve_prob, 2 * t + h + 1)
                    c = slice(1024 * h, 1024 * (h + 1))
                    dve.transpose(turned[:, c], pr[:, c]).then_inc(dve_turned, 1)

                if prev:
                    for i in range(KT) if not cur else range(1, KT) if nxt else ():
                        attended_lo(i)
                if cur:
                    if later(t):
                        dve.wait_ge(pe_x, 4 * (t - 1))
                    elif not prev:
                        dve.wait_ge(st_u[1], 32)
                    turn(0)
                    turn(1)
                if cur:
                    for h in range(2):
                        dve.wait_ge(dve_turned, 2 * t + h + 1)
                        c = slice(1024 * h, 1024 * (h + 1))
                        for q in range(DQ if prev else Q - 1):
                            p = slice(32 * q, 32 * (q + 1))
                            last = dve.tensor_copy(bd[p, q, c], turned[p, c])
                        last.then_inc(dve_bp, 1)
                if prev:
                    if not nxt:
                        dve.wait_ge(pe_x, 4 * (t - 1))
                    if cur:
                        dve.wait_ge(act_bp, 2 * (t + 1))
                        dve.wait_ge(dve_bp, 2 * (t + 1))
                    for m in range(4):
                        dve.wait_ge(pe_o, 4 * (t - 1) + m + 1)
                        for q in range(Q):
                            last = dve.scalar_tensor_tensor(out=x1_v[:, m, q, :], in0=w_bank(m)[:, q * N:(q + 1) * N],
                                                            scalar=factor((r + 2) % 3, DO, m, q),
                                                            in1=xtb_v[:, (r + 2) % 3, m, q, :],
                                                            op0=ALU.mult, op1=ALU.add)
                        last.then_inc(dve_x1, 1)
                if nxt:
                    dve.wait_ge(k_moved, 64 * (4 - GD) * (t + 1))
                    dve.wait_ge(k_moved_pool, 64 * GD * (t + 1))
                    dve.wait_ge(pe_v, 4 * (t + 1))
                    dve.tensor_copy(kp[:, :, :, :].rearrange("p c e g -> p e c g"), kq_v).then_inc(dve_kp, 1)
                if prev:
                    for b in range(Q):
                        p = slice(KP * b, KP * (b + 1))
                        dve.wait_ge(act_z, 4 * (t - 1) + b + 1)
                        dve.scalar_tensor_tensor(out=z[z_rows(b, 1), b // 2, :], in0=w_bank(0)[p, 0:N],
                                                 scalar=ub_st[p, (r + 2) % 3:(r + 2) % 3 + 1],
                                                 in1=z[z_rows(b, 0), b // 2, :].bitcast(f32),
                                                 op0=ALU.add, op1=ALU.subtract).then_inc(dve_zlo, 1)
                if prev:
                    for b in range(Q):
                        dve.wait_ge(pe_x, 4 * (t - 1) + b + 1)
                        dve.wait_ge(act_y, 4 * (t - 1) + b + 1)
                        dve.tensor_tensor(yb_v[:, b, :], g_bank(b), yb_v[:, b, :], ALU.add).then_inc(dve_out, 1)

            steps(dve, body)


_INS = ['x', 'cond_512', 'L0_cond_k_aff_w', 'L0_cond_k_aff_b', 'L0_cond_k_w', 'L0_cond_k_b', 'L0_cond_o_aff_w',
        'L0_cond_o_aff_b', 'L0_cond_o_w', 'L0_cond_o_b', 'L1_cond_W_dec', 'L1_cond_b_dec', 'L1_cond_V']


def kernel(**inputs):
    import numpy as _np
    import concourse.bacc as _bacc
    from concourse import mybir as _mybir
    from concourse.bass_utils import run_bass_kernel_spmd as _run

    nc = _bacc.Bacc("TRN2", target_bir_lowering=False, num_devices=1)
    arrays, args = {}, []
    for name in _INS:
        a = _np.ascontiguousarray(inputs[name])
        arrays[f"in_{name}_dram"] = a
        args.append(nc.dram_tensor(f"in_{name}_dram", a.shape, _mybir.dt.from_np(a.dtype), kind="ExternalInput").ap())
    shape = inputs['x'].shape
    args.append(nc.dram_tensor("out_0_dram", shape, _mybir.dt.float32, kind="ExternalOutput").ap())
    cond_resid_kernel(nc, *args)
    r = _run(nc, [arrays], core_ids=[0])
    return r.results[0]["out_0_dram"]
```
